# Optimizing a Trainium2 kernel written in Bass

```python
import numpy as np
import jax
import jax.numpy as jnp

def _softmax(x, axis=-1):
    return jax.nn.softmax(x, axis=axis)

def _gelu(x):
    return jax.nn.gelu(x, approximate=True)

def _silu(x):
    return jax.nn.silu(x)

def _sigmoid(x):
    return jax.nn.sigmoid(x)

def _layernorm(x, axis=-1, eps=1e-05):
    m = jnp.mean(x, axis=axis, keepdims=True)
    v = jnp.var(x, axis=axis, keepdims=True)
    return (x - m) / jnp.sqrt(v + eps)

def _scatter_add(tgt, idx, src, axis=0):
    return tgt.at[idx].add(src)

def _segment_sum(src, seg, n):
    return jax.ops.segment_sum(src, seg, n)
kernel_name = 'mk_xattn_ffn_d1_seqx_r8_5e5ba4'

def setup_inputs(seed: int=0):
    np.random.seed(seed)
    _w = jnp.asarray

    def _rec_inputs():
        import jax
        import jax.numpy as jnp
        _rk = jax.random.key(seed)
        x = 0.5 + 0.2887 * jax.random.normal(jax.random.fold_in(_rk, 1), (4, 256, 256), jnp.float32)
        _lenS = 256 - jax.random.randint(jax.random.fold_in(_rk, 7), (4,), 0, max(1, 256 // 4) + 1, jnp.int32)
        _lenS2 = 256 - jax.random.randint(jax.random.fold_in(_rk, 8), (4,), 0, max(1, 256 // 4) + 1, jnp.int32)
        _ctx_512P = jax.random.normal(jax.random.fold_in(_rk, 11), (4, 16, 64), jnp.float32)
        _ctx_512c = jax.random.dirichlet(jax.random.fold_in(_rk, 511), 0.3 * jnp.ones((16,), jnp.float32), (4, 256))
        _ctx_512t = jnp.einsum('bsk,bkd->bsd', _ctx_512c, _ctx_512P)
        _ctx_512t = _ctx_512t * jax.lax.rsqrt(jnp.mean(jnp.square(_ctx_512t)) + 1e-12) * 0.953939
        ctx_512 = -0.000392918 + 0.999932 * (_ctx_512t + 0.3 * jax.random.normal(jax.random.fold_in(_rk, 611), (4, 256, 64), jnp.float32))
        return (x, ctx_512)
    x, ctx_512 = _rec_inputs()

    def _L0_xattn_setup():
        import jax, jax.numpy as jnp
        import numpy as np
        B, N, D = (16, 256, 64)
        H = 4
        TOP_K_RATIO = 0.3
        key = jax.random.key(seed)
        k1, k2, k3, k4 = jax.random.split(key, 4)
        h = jax.random.normal(k1, (B, N, D), dtype=jnp.float32)
        adj_raw = jax.random.uniform(k2, (B, N, N), dtype=jnp.float32)
        lim = 1.0 / np.sqrt(D)
        Wq = jax.random.uniform(k3, (D, D), minval=-lim, maxval=lim, dtype=jnp.float32)
        Wk = jax.random.uniform(k4, (D, D), minval=-lim, maxval=lim, dtype=jnp.float32)
        gamma_raw = jnp.float32(-0.85)
        return {'h': h, 'adj_raw': adj_raw, 'Wq': Wq, 'Wk': Wk, 'gamma_raw': gamma_raw}
    _L0_xattn_all = _L0_xattn_setup()
    _L0_xattn_in = {k: v for k, v in _L0_xattn_all.items() if k in ('Wq', 'Wk', 'gamma_raw')}
    del _L0_xattn_all

    def _L0_ffn_setup():
        import jax, jax.numpy as jnp
        import numpy as np
        NUM_EXPERTS = 8
        HIDDEN = 256
        INTER = 256
        TOP_K = 2
        key = jax.random.key(seed)
        ks = jax.random.split(key, 7)
        hidden_states = jax.random.normal(ks[0], (4, 256, HIDDEN), dtype=jnp.float32)
        gate_w = jax.random.normal(ks[1], (HIDDEN, NUM_EXPERTS), dtype=jnp.float32) * 0.02
        fc1_w = jax.random.normal(ks[2], (NUM_EXPERTS, HIDDEN, INTER), dtype=jnp.float32) * 0.02
        fc1_b = jnp.zeros((NUM_EXPERTS, INTER), dtype=jnp.float32)
        fc2_w = jax.random.normal(ks[3], (NUM_EXPERTS, INTER, HIDDEN), dtype=jnp.float32) * 0.02
        fc2_b = jnp.zeros((NUM_EXPERTS, HIDDEN), dtype=jnp.float32)
        alpha = jax.random.normal(ks[4], (NUM_EXPERTS,), dtype=jnp.float32)
        return {'hidden_states': hidden_states, 'gate_w': gate_w, 'fc1_w': fc1_w, 'fc1_b': fc1_b, 'fc2_w': fc2_w, 'fc2_b': fc2_b, 'alpha': alpha}
    _L0_ffn_all = _L0_ffn_setup()
    _L0_ffn_in = {k: v for k, v in _L0_ffn_all.items() if k in ('gate_w', 'fc1_w', 'fc1_b', 'fc2_w', 'fc2_b', 'alpha')}
    del _L0_ffn_all
    return {'x': x, 'ctx_512': ctx_512, 'L0_xattn_Wq': _L0_xattn_in['Wq'], 'L0_xattn_Wk': _L0_xattn_in['Wk'], 'L0_xattn_gamma_raw': _L0_xattn_in['gamma_raw'], 'L0_ffn_gate_w': _L0_ffn_in['gate_w'], 'L0_ffn_fc1_w': _L0_ffn_in['fc1_w'], 'L0_ffn_fc1_b': _L0_ffn_in['fc1_b'], 'L0_ffn_fc2_w': _L0_ffn_in['fc2_w'], 'L0_ffn_fc2_b': _L0_ffn_in['fc2_b'], 'L0_ffn_alpha': _L0_ffn_in['alpha']}

def reference(x, ctx_512, L0_xattn_Wq, L0_xattn_Wk, L0_xattn_gamma_raw, L0_ffn_gate_w, L0_ffn_fc1_w, L0_ffn_fc1_b, L0_ffn_fc2_w, L0_ffn_fc2_b, L0_ffn_alpha):
    import jax
    import jax.numpy as jnp

    def _L0_xattn_ref(h, adj_raw, Wq, Wk, gamma_raw):
        import jax, jax.numpy as jnp
        import numpy as np
        B, N, D = (16, 256, 64)
        H = 4
        TOP_K_RATIO = 0.3
        b, n, dm = h.shape
        d = dm // H
        Q = (h @ Wq.T).reshape(b, n, H, d).transpose(0, 2, 1, 3)
        K = (h @ Wk.T).reshape(b, n, H, d).transpose(0, 2, 1, 3)
        sim = jnp.einsum('bhnd,bhmd->bnm', Q, K) / (jnp.sqrt(jnp.float32(d)) * H)
        k = max(1, int(n * TOP_K_RATIO))
        topk_vals = jax.lax.top_k(sim, k)[0]
        threshold = topk_vals[:, :, -1:]
        sparse_mask = (sim >= threshold).astype(sim.dtype)
        A_learned = jax.nn.sigmoid(sim) * sparse_mask
        A_learned = (A_learned + jnp.swapaxes(A_learned, -1, -2)) * 0.5
        gamma = jax.nn.sigmoid(gamma_raw)
        return (1.0 - gamma) * adj_raw + gamma * A_learned

    def _L0_ffn_ref(hidden_states, gate_w, fc1_w, fc1_b, fc2_w, fc2_b, alpha):
        import jax, jax.numpy as jnp
        import numpy as np
        NUM_EXPERTS = 8
        HIDDEN = 256
        INTER = 256
        TOP_K = 2
        B, S, H = hidden_states.shape
        x = hidden_states.reshape(-1, H)
        probs = jax.nn.softmax(x @ gate_w, axis=-1)
        gate_score, gate_idx = jax.lax.top_k(probs, TOP_K)
        gate_score = gate_score / jnp.sum(gate_score, axis=-1, keepdims=True)
        onehot = jax.nn.one_hot(gate_idx, NUM_EXPERTS, dtype=x.dtype)
        combine = jnp.einsum('tk,tke->te', gate_score, onehot) * alpha[None, :]
        h = jnp.einsum('th,ehi->eti', x, fc1_w) + fc1_b[:, None, :]
        h = jax.nn.gelu(h, approximate=False)
        y = jnp.einsum('eti,eih->eth', h, fc2_w) + fc2_b[:, None, :]
        out = jnp.einsum('eth,te->th', y, combine)
        return out.reshape(B, S, H)
    x = x + _L0_xattn_ref(ctx_512, _layernorm(x, axis=-1), L0_xattn_Wq, L0_xattn_Wk, L0_xattn_gamma_raw)
    x = x + _L0_ffn_ref(_layernorm(x, axis=-1), L0_ffn_gate_w, L0_ffn_fc1_w, L0_ffn_fc1_b, L0_ffn_fc2_w, L0_ffn_fc2_b, L0_ffn_alpha)
    return x

_drawn_inputs = setup_inputs


def setup_inputs(seed=0):
    import zlib

    import numpy as np

    out = dict(_drawn_inputs(seed))
    spreads = {'L0_ffn_fc1_b': (0.0, 0.66), 'L0_ffn_fc2_b': (0.0, 0.1)}
    factors = {}
    for name, (base, spread) in spreads.items():
        noise = np.random.default_rng([zlib.crc32(name.encode()), seed]).standard_normal(out[name].shape)
        drawn = base * np.exp(spread * noise) if base else spread * noise
        out[name] = jnp.asarray(drawn.astype(out[name].dtype))
    for name, factor in factors.items():
        out[name] = (out[name] * factor).astype(out[name].dtype)
    return out
```

```python
from contextlib import ExitStack

import concourse.bass as bass
from concourse import mybir

P = 128
ALU = mybir.AluOpType
ACT = mybir.ActivationFunctionType
F32 = mybir.dt.float32
F32R = mybir.dt.float32r
U32 = mybir.dt.uint32

TOP_K_RATIO = 0.3
HEADS = 4
LN_EPS = 1e-5
REPLACED = -3.0e38
MASK_STEP, XN_STEP = 6, 7
LAG = 2


def xattn_moe_program(nc, x, ctx_t, wq, wk, gamma, gate_w, w1, b1, w2, b2, alpha, identity, iota, out):
    HID = x.shape[2]
    D, TOKENS = ctx_t.shape
    EXPERTS = w1.shape[1]
    N = HID
    BATCHES = TOKENS // N
    TILES = N // P
    CH = HID // P
    STEPS = BATCHES * EXPERTS
    SIM_SCALE = 1.0 / ((D // HEADS) ** 0.5 * HEADS)
    TOP_K = max(1, int(N * TOP_K_RATIO))
    ROUNDS = (TOP_K + 7) // 8
    LAST = (TOP_K - 1) % 8

    with ExitStack() as ctx:
        def sb(name, shape, dt=F32):
            return ctx.enter_context(nc.sbuf_tensor(name, shape, dt))

        def bank(name):
            return ctx.enter_context(nc.psum_tensor(name, [P, 512], F32))

        def sem(name):
            return ctx.enter_context(nc.semaphore(name))

        ctx_sb = sb("ctx_sb", [D, TOKENS])
        wq_sb = sb("wq_sb", [D, D])
        wk_sb = sb("wk_sb", [D, D])
        x_sb = sb("x_sb", [P, BATCHES, TILES, HID])
        gamma_sb = sb("gamma_sb", [P, 1])
        alpha_sb = sb("alpha_sb", [P, EXPERTS])
        gate_sb = sb("gate_sb", [P, CH, EXPERTS])
        w1_sb = sb("w1_sb", [P, EXPERTS, CH, HID])
        w2_sb = sb("w2_sb", [P, EXPERTS, CH, HID])
        b1_sb = sb("b1_sb", [P, EXPERTS, CH])
        b2_sb = sb("b2_sb", [EXPERTS, HID])
        ident_sb = sb("ident_sb", [P, P])
        iota_sb = sb("iota_sb", [P, EXPERTS])
        gate_hi = sb("gate_hi", [P, CH, EXPERTS], F32R)
        gate_lo = sb("gate_lo", [P, CH, EXPERTS], F32R)
        w1_hi = sb("w1_hi", [P, EXPERTS, CH, HID], F32R)
        w1_lo = sb("w1_lo", [P, EXPERTS, CH, HID], F32R)
        w2_hi = sb("w2_hi", [P, EXPERTS, CH, HID], F32R)
        w2_lo = sb("w2_lo", [P, EXPERTS, CH, HID], F32R)
        m_sb = sb("m_sb", [D, D])
        u_sb = sb("u_sb", [D, TOKENS])
        sim = sb("sim", [P, BATCHES, TILES, N])
        left = sb("left", [P, TILES, N])
        top8 = sb("top8", [P, TILES, 8])
        half = sb("half", [P, BATCHES, TILES, N])
        gam = sb("gam", [P, 4])
        stats = sb("stats", [P, TILES, 6])
        mv1 = sb("mv1", [P, BATCHES, TILES, 2])
        veps1 = sb("veps1", [P, BATCHES, TILES])
        rstd1 = sb("rstd1", [P, BATCHES, TILES])
        mul1 = sb("mul1", [P, BATCHES, TILES])
        add1 = sb("add1", [P, BATCHES, TILES])
        stats2 = sb("stats2", [P, TILES, 6])
        mv2 = sb("mv2", [P, BATCHES, TILES, 2])
        veps2 = sb("veps2", [P, BATCHES, TILES])
        rstd2 = sb("rstd2", [P, BATCHES, TILES])
        neg_half = sb("neg_half", [P, TILES])
        x1 = sb("x1", [P, BATCHES, TILES, HID])
        xn = sb("xn", [P, TILES, HID])
        xt_hi = sb("xt_hi", [P, 2, CH, N], F32R)
        xt_lo = sb("xt_lo", [P, 2, CH, N], F32R)
        logits = sb("logits", [P, TILES, EXPERTS])
        best = sb("best", [P, TILES, 8])
        best_at = sb("best_at", [P, TILES, 8], U32)
        best_f = sb("best_f", [P, TILES, 2])
        gap = sb("gap", [P, TILES])
        gap_th = sb("gap_th", [P, TILES])
        score = sb("score", [P, 2, TILES])
        pick = sb("pick", [P, 2, TILES, EXPERTS])
        comb = sb("comb", [P, BATCHES, TILES, EXPERTS])
        comb_t = sb("comb_t", [EXPERTS, TILES, P])
        h_act = sb("h_act", [P, 2, CH, N])
        h_hi = sb("h_hi", [P, LAG + 1, CH, N], F32R)
        h_lo = sb("h_lo", [P, LAG + 1, CH, N], F32R)
        acc = sb("acc", [P, 2, TILES, HID])

        p_h = [bank("p_h0"), bank("p_h1")]
        p_y = [bank("p_y0"), bank("p_y1")]
        p_s = bank("p_s")
        p_a = bank("p_a")
        p_x = bank("p_x")
        p_g = bank("p_g")

        def tiled(b):
            return b[:, :].rearrange("p (t n) -> p t n", t=TILES)

        attn_in = sem("attn_in")
        x_in = [sem(f"x_in{b}") for b in range(BATCHES)]
        small_in = sem("small_in")
        w1_in = [sem(f"w1_in{e}") for e in range(EXPERTS)]
        w2_in = [sem(f"w2_in{e}") for e in range(EXPERTS)]
        out_done = [sem(f"out_done{b}") for b in range(BATCHES)]
        m_ready = sem("m_ready")
        m_copied = sem("m_copied")
        u_ready = sem("u_ready")
        u_copied = sem("u_copied")
        sim_ready = sem("sim_ready")
        sim_copied = sem("sim_copied")
        gam_th = sem("gam_th")
        gam_ready = sem("gam_ready")
        sig_th = sem("sig_th")
        sig_ready = sem("sig_ready")
        search = sem("search")
        masked = sem("masked")
        masked_t = sem("masked_t")
        ln1_stats = sem("ln1_stats")
        ln1_agg = sem("ln1_agg")
        ln1_veps = sem("ln1_veps")
        ln1_rstd = sem("ln1_rstd")
        ln1_mul = sem("ln1_mul")
        base_ready = sem("base_ready")
        base_sum = sem("base_sum")
        x1_ready = sem("x1_ready")
        ln2_stats = sem("ln2_stats")
        ln2_agg = sem("ln2_agg")
        ln2_veps = sem("ln2_veps")
        ln2_rstd = sem("ln2_rstd")
        xn_ready = sem("xn_ready")
        xn_t = sem("xn_t")
        xt_hi_ready = sem("xt_hi_ready")
        xt_lo_ready = sem("xt_lo_ready")
        gate_hi_ready = sem("gate_hi_ready")
        gate_lo_ready = sem("gate_lo_ready")
        logits_ready = sem("logits_ready")
        gating = sem("gating")
        gap_ready = sem("gap_ready")
        gap_th_ready = sem("gap_th_ready")
        comb_ready = sem("comb_ready")
        comb_tr = sem("comb_tr")
        comb_t_ready = sem("comb_t_ready")
        b2_ready = sem("b2_ready")
        acc_init = sem("acc_init")
        const_set = sem("const_set")
        w1_hi_ready = sem("w1_hi_ready")
        w1_lo_ready = sem("w1_lo_ready")
        w2_hi_ready = sem("w2_hi_ready")
        w2_lo_ready = sem("w2_lo_ready")
        h_ready = sem("h_ready")
        h_act_ready = sem("h_act_ready")
        h_hi_ready = sem("h_hi_ready")
        h_lo_ready = sem("h_lo_ready")
        y_ready = sem("y_ready")
        y_added = sem("y_added")

        block = ctx.enter_context(nc.Block())

        @block.sync
        def _(sp):
            sp.dma_start(wq_sb[:], wq).then_inc(attn_in, 16)
            sp.dma_start(wk_sb[:], wk).then_inc(attn_in, 16)
            sp.dma_start(ctx_sb[:], ctx_t).then_inc(attn_in, 16)
            sp.dma_start(x_sb[:, 0], x[:, 0:TILES]).then_inc(x_in[0], 16)
            for dst, src in ((gamma_sb, gamma), (ident_sb, identity), (gate_sb, gate_w), (iota_sb, iota),
                             (alpha_sb, alpha), (b1_sb, b1), (b2_sb, b2)):
                sp.dma_start(dst[:], src).then_inc(small_in, 16)
            for e in range(EXPERTS):
                sp.dma_start(w1_sb[:, e], w1[:, e]).then_inc(w1_in[e], 16)
                sp.dma_start(w2_sb[:, e], w2[:, e]).then_inc(w2_in[e], 16)
                if e == 1:
                    for b in range(1, BATCHES):
                        sp.dma_start(x_sb[:, b], x[:, b * TILES:(b + 1) * TILES]).then_inc(x_in[b], 16)
            for b in range(BATCHES):
                sp.wait_ge(y_added, (b + 1) * EXPERTS)
                sp.dma_start(out[:, b * TILES:(b + 1) * TILES], acc[:, b % 2]).then_inc(out_done[b], 16)
            for b in range(BATCHES):
                sp.wait_ge(out_done[b], 16)

        SMALL_IN = 16 * 7

        @block.tensor
        def _(pe):
            def similarities():
                pe.wait_ge(attn_in, 48)
                nc.tensor.matmul(p_g[0:D, 0:D], wq_sb[:], wk_sb[:], start=True, stop=True).then_inc(m_ready, 1)
                pe.wait_ge(m_copied, 1)
                for b in range(BATCHES):
                    dst = (p_a, p_x, p_y[0], p_y[1])[b]
                    nc.tensor.matmul(dst[0:D, 0:N], m_sb[:], ctx_sb[:, b * N:(b + 1) * N], start=True,
                                     stop=True).then_inc(u_ready, 1)
                    if b == 0:
                        sim_of(0)
                for b in range(1, BATCHES):
                    sim_of(b)

            def sim_of(b):
                pe.wait_ge(u_copied, b + 1)
                dst = tiled((p_s, p_h[0], p_h[1], p_g)[b])
                for t in range(TILES):
                    n0 = b * N + t * P
                    last = nc.tensor.matmul(dst[:, t, :], u_sb[:, n0:n0 + P], ctx_sb[:, b * N:(b + 1) * N],
                                            start=True, stop=True)
                last.then_inc(sim_ready, 1)

            def transpose_masked(b):
                pe.wait_ge(masked, b + 1)
                if b == 0:
                    pe.wait_ge(small_in, SMALL_IN)
                    pe.wait_ge(u_copied, BATCHES)
                else:
                    pe.wait_ge(acc_init, b)
                for t in range(TILES):
                    for r in range(TILES):
                        last = nc.tensor.transpose(tiled(p_a)[:, t, r * P:(r + 1) * P],
                                                   half[:, b, r, t * P:(t + 1) * P], ident_sb[:])
                last.then_inc(masked_t, 1)

            def transpose_xn(b):
                pe.wait_ge(xn_ready, b + 1)
                if b >= 1:
                    pe.wait_ge(xt_lo_ready, b)
                for k in range(CH):
                    for t in range(TILES):
                        last = nc.tensor.transpose(tiled(p_x)[:, k, t * P:(t + 1) * P],
                                                   xn[:, t, k * P:(k + 1) * P], ident_sb[:])
                last.then_inc(xn_t, 1)

            def gate(b):
                if b == 0:
                    pe.wait_ge(gate_lo_ready, 1)
                    pe.wait_ge(sim_copied, BATCHES)
                else:
                    pe.wait_ge(comb_t_ready, b)
                for t in range(TILES):
                    dst = p_g[:, t * EXPERTS:(t + 1) * EXPERTS]
                    pairs = [(xh, g, k) for k in range(CH) for xh in (xt_hi, xt_lo) for g in (gate_hi, gate_lo)]
                    for n, (xh, g, k) in enumerate(pairs):
                        last = nc.tensor.matmul(dst, xh[:, b % 2, k, t * P:(t + 1) * P], g[:, k, :],
                                                start=n == 0, stop=n == len(pairs) - 1)
                last.then_inc(logits_ready, 1)

            def transpose_comb(b):
                pe.wait_ge(comb_ready, b + 1)
                for t in range(TILES):
                    last = nc.tensor.transpose(p_g[0:EXPERTS, 64 + t * P:64 + (t + 1) * P], comb[:, b, t, :],
                                               ident_sb[:])
                last.then_inc(comb_tr, 1)

            def bias_sums(b):
                pe.wait_ge(comb_t_ready, b + 1)
                pe.wait_ge(x1_ready, b + 1)
                for t in range(TILES):
                    last = nc.tensor.matmul(tiled(p_a)[:, t, :], comb_t[:, t, :], b2_sb[:], start=True, stop=True)
                last.then_inc(b2_ready, 1)

            def up(s):
                b, e = divmod(s, EXPERTS)
                if e == 0:
                    pe.wait_ge(xt_lo_ready, b + 1)
                if b == 0:
                    pe.wait_ge(w1_lo_ready, e + 1)
                if s >= 2:
                    pe.wait_ge(h_act_ready, s - 1)
                else:
                    pe.wait_ge(sim_copied, BATCHES)
                for c in range(CH):
                    dst = tiled(p_h[s % 2])[:, c, :]
                    trio = [(w, v, k) for w, v in ((w1_hi, xt_hi), (w1_lo, xt_hi), (w1_hi, xt_lo)) for k in range(CH)]
                    for n, (w, v, k) in enumerate(trio):
                        last = nc.tensor.matmul(dst, w[:, e, k, c * P:(c + 1) * P], v[:, b % 2, k, :],
                                                start=n == 0, stop=n == len(trio) - 1)
                last.then_inc(h_ready, 1)

            def down(s):
                b, e = divmod(s, EXPERTS)
                pe.wait_ge(h_lo_ready, s + 1)
                if b == 0:
                    pe.wait_ge(w2_lo_ready, e + 1)
                if s >= 2:
                    pe.wait_ge(y_added, s - 1)
                else:
                    pe.wait_ge(u_copied, BATCHES)
                for t in range(TILES):
                    dst = tiled(p_y[s % 2])[:, t, :]
                    trio = [(v, w, k) for v, w in ((h_hi, w2_hi), (h_hi, w2_lo), (h_lo, w2_hi)) for k in range(CH)]
                    for n, (v, w, k) in enumerate(trio):
                        last = nc.tensor.matmul(dst, v[:, s % (LAG + 1), k, t * P:(t + 1) * P], w[:, e, k, :],
                                                start=n == 0, stop=n == len(trio) - 1)
                last.then_inc(y_ready, 1)

            similarities()
            transpose_masked(0)
            transpose_xn(0)
            for s in range(STEPS + LAG):
                b, e = divmod(s, EXPERTS)
                if s < STEPS:
                    if e == 0:
                        pe.wait_ge(xt_lo_ready, b + 1)
                        gate(b)
                    up(s)
                if s < STEPS and e == 1:
                    transpose_comb(b)
                if s >= LAG:
                    down(s - LAG)
                if s < STEPS and e == 1:
                    bias_sums(b)
                if e == MASK_STEP and b + 1 < BATCHES:
                    transpose_masked(b + 1)
                if e == XN_STEP and b + 1 < BATCHES:
                    transpose_xn(b + 1)

        @block.scalar
        def _(act):
            def sim_copy(b):
                act.wait_ge(sim_ready, b + 1)
                nc.scalar.activation(sim[:, b], tiled((p_s, p_h[0], p_h[1], p_g)[b]), ACT.Copy).then_inc(sim_copied, 1)

            def u_copy(b):
                act.wait_ge(u_ready, b + 1)
                nc.scalar.activation(u_sb[:, b * N:(b + 1) * N], (p_a, p_x, p_y[0], p_y[1])[b][0:D, 0:N], ACT.Copy,
                                     scale=SIM_SCALE).then_inc(u_copied, 1)

            def sigmoid(b):
                act.wait_ge(sim_copied, b + 1)
                nc.scalar.activation(half[:, b], sim[:, b], ACT.Tanh, scale=0.5).then_inc(sig_th, 1)
                act.wait_ge(sig_th, b + 1)
                if b == 0:
                    act.wait_ge(gam_ready, 1)
                nc.scalar.activation(half[:, b], half[:, b], ACT.Identity, scale=gam[:, 1:2],
                                     bias=gam[:, 1:2]).then_inc(sig_ready, 1)

            def weight_hi(e, dst, src, arrived, ready):
                act.wait_ge(arrived[e], 16)
                nc.scalar.activation(dst[:, e], src[:, e], ACT.Copy).then_inc(ready, 1)

            def xt_hi_of(b):
                act.wait_ge(xn_t, b + 1)
                if b >= 2:
                    act.wait_ge(h_ready, (b - 1) * EXPERTS)
                nc.scalar.activation(xt_hi[:, b % 2], tiled(p_x), ACT.Copy).then_inc(xt_hi_ready, 1)

            def gelu(s):
                b, e = divmod(s, EXPERTS)
                act.wait_ge(h_ready, s + 1)
                if s >= 2:
                    act.wait_ge(h_lo_ready, s - 1)
                for c in range(CH):
                    last = nc.scalar.activation(h_act[:, s % 2, c], tiled(p_h[s % 2])[:, c, :], ACT.Gelu,
                                                bias=b1_sb[:, e, c:c + 1])
                last.then_inc(h_act_ready, 1)

            def hidden_hi(s):
                act.wait_ge(h_act_ready, s + 1)
                if s > LAG:
                    act.wait_ge(y_ready, s - LAG)
                nc.scalar.activation(h_hi[:, s % (LAG + 1)], h_act[:, s % 2], ACT.Copy).then_inc(h_hi_ready, 1)

            act.wait_ge(m_ready, 1)
            nc.scalar.activation(m_sb[:], p_g[0:D, 0:D], ACT.Copy).then_inc(m_copied, 1)
            u_copy(0)
            sim_copy(0)
            for b in range(1, BATCHES):
                u_copy(b)
            act.wait_ge(small_in, SMALL_IN)
            nc.scalar.activation(gam[:, 0:1], gamma_sb[:], ACT.Tanh, scale=0.5).then_inc(gam_th, 1)
            nc.scalar.activation(gate_hi[:], gate_sb[:], ACT.Copy).then_inc(gate_hi_ready, 1)
            for b in range(1, BATCHES):
                sim_copy(b)
            sigmoid(0)
            for e in range(EXPERTS):
                weight_hi(e, w1_hi, w1_sb, w1_in, w1_hi_ready)
                weight_hi(e, w2_hi, w2_sb, w2_in, w2_hi_ready)
            for b in range(1, BATCHES):
                sigmoid(b)
            xt_hi_of(0)
            for s in range(STEPS):
                b, e = divmod(s, EXPERTS)
                gelu(s)
                hidden_hi(s)
                if e == 0:
                    act.wait_ge(gap_ready, b + 1)
                    nc.scalar.activation(gap_th[:], gap[:], ACT.Tanh, scale=0.5).then_inc(gap_th_ready, 1)
                if e == XN_STEP and b + 1 < BATCHES:
                    xt_hi_of(b + 1)

        @block.gpsimd
        def _(pool):
            def rstd(mv, veps, rs, b, agg, veps_ready, ready):
                pool.wait_ge(agg, b + 1)
                nc.gpsimd.tensor_scalar(veps[:, b, :], mv[:, b, :, 1], LN_EPS, 1.0, ALU.add, ALU.mult).then_inc(
                    veps_ready, 1)
                pool.wait_ge(veps_ready, b + 1)
                nc.gpsimd.tensor_tensor(rs[:, b, :], veps[:, b, :], neg_half[:], ALU.pow).then_inc(ready, 1)

            def weight_lo(e, dst, raw, hi, hi_ready, ready):
                pool.wait_ge(hi_ready, e + 1)
                nc.gpsimd.tensor_tensor(dst[:, e], raw[:, e], hi[:, e], ALU.subtract).then_inc(ready, 1)

            def base(b):
                pool.wait_ge(ln1_mul, b + 1)
                for t in range(TILES):
                    last = nc.gpsimd.tensor_scalar(x_sb[:, b, t], x_sb[:, b, t], mul1[:, b, t:t + 1],
                                                   add1[:, b, t:t + 1], ALU.mult, ALU.add)
                last.then_inc(base_ready, 1)

            def add_masked(b):
                pool.wait_ge(masked, b + 1)
                pool.wait_ge(base_ready, b + 1)
                nc.gpsimd.tensor_tensor(x_sb[:, b], x_sb[:, b], half[:, b], ALU.add).then_inc(base_sum, 1)

            nc.gpsimd.memset(neg_half[:], -0.5).then_inc(const_set, 1)
            pool.wait_ge(const_set, 1)
            rstd(mv1, veps1, rstd1, 0, ln1_agg, ln1_veps, ln1_rstd)
            pool.wait_ge(gate_hi_ready, 1)
            nc.gpsimd.tensor_tensor(gate_lo[:], gate_sb[:], gate_hi[:], ALU.subtract).then_inc(gate_lo_ready, 1)
            base(0)
            for e in range(2):
                weight_lo(e, w1_lo, w1_sb, w1_hi, w1_hi_ready, w1_lo_ready)
                weight_lo(e, w2_lo, w2_sb, w2_hi, w2_hi_ready, w2_lo_ready)
            for b in range(1, BATCHES):
                rstd(mv1, veps1, rstd1, b, ln1_agg, ln1_veps, ln1_rstd)
            add_masked(0)
            for e in range(2, 4):
                weight_lo(e, w1_lo, w1_sb, w1_hi, w1_hi_ready, w1_lo_ready)
                weight_lo(e, w2_lo, w2_sb, w2_hi, w2_hi_ready, w2_lo_ready)
            rstd(mv2, veps2, rstd2, 0, ln2_agg, ln2_veps, ln2_rstd)
            for s in range(STEPS):
                b, e = divmod(s, EXPERTS)
                if b == 0 and e >= 4:
                    weight_lo(e, w1_lo, w1_sb, w1_hi, w1_hi_ready, w1_lo_ready)
                    weight_lo(e, w2_lo, w2_sb, w2_hi, w2_hi_ready, w2_lo_ready)
                pool.wait_ge(h_hi_ready, s + 1)
                if s > LAG:
                    pool.wait_ge(y_ready, s - LAG)
                nc.gpsimd.tensor_tensor(h_lo[:, s % (LAG + 1)], h_act[:, s % 2], h_hi[:, s % (LAG + 1)],
                                        ALU.subtract).then_inc(h_lo_ready, 1)
                if b + 1 < BATCHES:
                    if e == 1:
                        base(b + 1)
                    if e == MASK_STEP:
                        add_masked(b + 1)
                    if e == XN_STEP:
                        rstd(mv2, veps2, rstd2, b + 1, ln2_agg, ln2_veps, ln2_rstd)

        @block.vector
        def _(dve):
            def ln1(b):
                dve.wait_ge(x_in[b], 16)
                if b:
                    dve.wait_ge(ln1_agg, b)
                for t in range(TILES):
                    last = nc.vector.bn_stats(stats[:, t, :], x_sb[:, b, t])
                last.then_inc(ln1_stats, 1)
                dve.wait_ge(ln1_stats, b + 1)
                for t in range(TILES):
                    last = nc.vector.bn_aggr(mv1[:, b, t, :], stats[:, t, :])
                last.then_inc(ln1_agg, 1)

            def ln1_affine(b):
                dve.wait_ge(ln1_rstd, b + 1)
                nc.vector.tensor_scalar(mul1[:, b, :], rstd1[:, b, :], gam[:, 2:3], 1.0, ALU.mult, ALU.add)
                nc.vector.scalar_tensor_tensor(add1[:, b, :], mv1[:, b, :, 0], gam[:, 3:4], rstd1[:, b, :], ALU.mult,
                                               ALU.mult).then_inc(ln1_mul, 1)

            def gamma_terms():
                dve.wait_ge(gam_th, 1)
                nc.vector.tensor_scalar(gam[:, 1:2], gam[:, 0:1], 0.125, 0.125, ALU.mult, ALU.add)
                nc.vector.tensor_scalar(gam[:, 2:3], gam[:, 0:1], -0.5, 0.5, ALU.mult, ALU.add)
                nc.vector.tensor_scalar(gam[:, 3:4], gam[:, 0:1], 0.5, -0.5, ALU.mult, ALU.add).then_inc(gam_ready, 1)
                dve.wait_ge(gam_ready, 1)

            searched = [0]

            def search_rounds(b, rounds):
                for r in rounds:
                    for t in range(TILES):
                        if r > 0:
                            dve.wait_ge(search, searched[0] - TILES + 1)
                        elif b > 0:
                            dve.wait_ge(masked, b)
                        src = sim[:, b, t] if r == 0 else left[:, t]
                        nc.vector.max(top8[:, t], src).then_inc(search, 1)
                        searched[0] += 1
                    if r == ROUNDS - 1:
                        return
                    for t in range(TILES):
                        dve.wait_ge(search, searched[0] - TILES + 1)
                        src = sim[:, b, t] if r == 0 else left[:, t]
                        nc.vector.match_replace(left[:, t], top8[:, t], src, REPLACED).then_inc(search, 1)
                        searched[0] += 1

            def mask(b):
                dve.wait_ge(search, searched[0])
                dve.wait_ge(sig_ready, b + 1)
                for t in range(TILES):
                    last = nc.vector.scalar_tensor_tensor(half[:, b, t], sim[:, b, t], top8[:, t, LAST:LAST + 1],
                                                          half[:, b, t], ALU.is_ge, ALU.mult)
                last.then_inc(masked, 1)

            def residual(b):
                dve.wait_ge(masked_t, b + 1)
                dve.wait_ge(base_sum, b + 1)
                nc.vector.tensor_tensor(x1[:, b], x_sb[:, b], tiled(p_a), ALU.add).then_inc(x1_ready, 1)
                dve.wait_ge(x1_ready, b + 1)
                for t in range(TILES):
                    last = nc.vector.bn_stats(stats2[:, t, :], x1[:, b, t])
                last.then_inc(ln2_stats, 1)
                dve.wait_ge(ln2_stats, b + 1)
                for t in range(TILES):
                    last = nc.vector.bn_aggr(mv2[:, b, t, :], stats2[:, t, :])
                last.then_inc(ln2_agg, 1)

            def normalise(b):
                dve.wait_ge(ln2_rstd, b + 1)
                if b:
                    dve.wait_ge(xn_t, b)
                for t in range(TILES):
                    last = nc.vector.tensor_scalar(xn[:, t], x1[:, b, t], mv2[:, b, t, 0:1], rstd2[:, b, t:t + 1],
                                                   ALU.subtract, ALU.mult)
                last.then_inc(xn_ready, 1)

            def xt_lo_of(b):
                dve.wait_ge(xt_hi_ready, b + 1)
                if b >= 2:
                    dve.wait_ge(h_ready, (b - 1) * EXPERTS)
                nc.vector.tensor_tensor(xt_lo[:, b % 2], tiled(p_x), xt_hi[:, b % 2], ALU.subtract).then_inc(
                    xt_lo_ready, 1)

            gated = [0]

            def step(ins):
                gated[0] += 1
                ins.then_inc(gating, 1)

            def settle():
                dve.wait_ge(gating, gated[0])

            def top2(b):
                dve.wait_ge(logits_ready, b + 1)
                step(nc.vector.tensor_copy(logits[:], p_g[:, 0:TILES * EXPERTS].rearrange("p (t e) -> p t e", t=TILES)))
                settle()
                for t in range(TILES):
                    step(nc.vector.max(best[:, t], logits[:, t]))
                settle()
                nc.vector.tensor_tensor(gap[:], best[:, :, 0], best[:, :, 1], ALU.subtract).then_inc(gap_ready, 1)
                for t in range(TILES):
                    step(nc.vector.max_index(best_at[:, t], best[:, t], logits[:, t]))
                settle()
                step(nc.vector.tensor_copy(best_f[:], best_at[:, :, 0:2]))
                dve.wait_ge(gap_th_ready, b + 1)
                step(nc.vector.tensor_scalar(score[:, 0], gap_th[:], 0.5, 0.5, ALU.mult, ALU.add))
                step(nc.vector.tensor_scalar(score[:, 1], gap_th[:], -0.5, 0.5, ALU.mult, ALU.add))
                settle()
                for j in range(2):
                    for t in range(TILES):
                        step(nc.vector.tensor_scalar(pick[:, j, t], iota_sb[:], best_f[:, t, j:j + 1],
                                                     score[:, j, t:t + 1], ALU.is_equal, ALU.mult))
                settle()
                step(nc.vector.tensor_tensor(pick[:, 0], pick[:, 0], pick[:, 1], ALU.add))
                settle()
                for t in range(TILES):
                    last = nc.vector.tensor_tensor(comb[:, b, t], pick[:, 0, t], alpha_sb[:], ALU.mult)
                last.then_inc(comb_ready, 1)

            def comb_copy(b):
                dve.wait_ge(comb_tr, b + 1)
                nc.vector.tensor_copy(comb_t[:], p_g[0:EXPERTS, 64:64 + N].rearrange("e (t p) -> e t p", t=TILES)
                                      ).then_inc(comb_t_ready, 1)

            def start_acc(b):
                dve.wait_ge(b2_ready, b + 1)
                if b >= 2:
                    dve.wait_ge(out_done[b - 2], 16)
                nc.vector.tensor_tensor(acc[:, b % 2], x1[:, b], tiled(p_a), ALU.add).then_inc(acc_init, 1)
                dve.wait_ge(acc_init, b + 1)

            def add_expert(s):
                b, e = divmod(s, EXPERTS)
                dve.wait_ge(y_ready, s + 1)
                if e:
                    dve.wait_ge(y_added, s)
                for t in range(TILES):
                    last = nc.vector.scalar_tensor_tensor(acc[:, b % 2, t], tiled(p_y[s % 2])[:, t, :],
                                                          comb[:, b, t, e:e + 1], acc[:, b % 2, t], ALU.mult, ALU.add)
                last.then_inc(y_added, 1)

            CUT = [0, 2, 4, 6, 8, 10, 10, 10, 10]

            dve.wait_ge(sim_copied, 1)
            search_rounds(0, range(0, 2))
            gamma_terms()
            ln1(0)
            search_rounds(0, range(2, 6))
            ln1_affine(0)
            search_rounds(0, range(6, ROUNDS))
            mask(0)
            for b in range(1, BATCHES):
                ln1(b)
            residual(0)
            for b in range(1, BATCHES):
                ln1_affine(b)
            normalise(0)
            xt_lo_of(0)
            for s in range(STEPS + LAG):
                b, e = divmod(s, EXPERTS)
                nxt = b + 1
                if e == 0 and b < BATCHES:
                    top2(b)
                if e == 1 and b < BATCHES:
                    comb_copy(b)
                if s >= LAG:
                    if (s - LAG) % EXPERTS == 0:
                        start_acc((s - LAG) // EXPERTS)
                    add_expert(s - LAG)
                if nxt < BATCHES:
                    if e == 0:
                        dve.wait_ge(sim_copied, nxt + 1)
                    if CUT[e] < CUT[e + 1]:
                        search_rounds(nxt, range(CUT[e], CUT[e + 1]))
                    if e == MASK_STEP - 1:
                        mask(nxt)
                    if e == MASK_STEP:
                        residual(nxt)
                    if e == XN_STEP:
                        normalise(nxt)
                        xt_lo_of(nxt)


def kernel(x, ctx_512, L0_xattn_Wq, L0_xattn_Wk, L0_xattn_gamma_raw, L0_ffn_gate_w, L0_ffn_fc1_w, L0_ffn_fc1_b,
           L0_ffn_fc2_w, L0_ffn_fc2_b, L0_ffn_alpha):
    import numpy as np
    import concourse.bacc as bacc
    from concourse.bass_utils import run_bass_kernel_spmd

    B, S, H = x.shape
    T = B * S // P
    E = L0_ffn_fc1_w.shape[0]
    C = H // P

    def rows(w):
        return np.asarray(w).reshape(E, C, P, -1).transpose(2, 0, 1, 3)

    arrays = {
        "x": np.asarray(x).reshape(T, P, H).transpose(1, 0, 2),
        "ctx_t": np.asarray(ctx_512).reshape(B * S, -1).T,
        "wq": np.asarray(L0_xattn_Wq),
        "wk": np.asarray(L0_xattn_Wk),
        "gamma": np.broadcast_to(np.asarray(L0_xattn_gamma_raw).reshape(1, 1), (P, 1)),
        "gate_w": np.asarray(L0_ffn_gate_w).reshape(C, P, E).transpose(1, 0, 2),
        "w1": rows(L0_ffn_fc1_w),
        "b1": np.asarray(L0_ffn_fc1_b).reshape(E, C, P).transpose(2, 0, 1),
        "w2": rows(L0_ffn_fc2_w),
        "b2": np.asarray(L0_ffn_fc2_b),
        "alpha": np.broadcast_to(np.asarray(L0_ffn_alpha)[None, :], (P, E)),
        "identity": np.eye(P, dtype=np.float32),
        "iota": np.broadcast_to(np.arange(E, dtype=np.float32)[None, :], (P, E)),
    }
    arrays = {k: np.ascontiguousarray(v) for k, v in arrays.items()}
    nc = bacc.Bacc("TRN2", target_bir_lowering=False, num_devices=1)
    aps = {k: nc.dram_tensor(k, v.shape, mybir.dt.from_np(v.dtype), kind="ExternalInput").ap()
           for k, v in arrays.items()}
    out = nc.dram_tensor("out", (P, T, H), F32, kind="ExternalOutput").ap()
    xattn_moe_program(nc, out=out, **aps)
    result = run_bass_kernel_spmd(nc, [arrays], core_ids=[0]).results[0]["out"]
    return np.ascontiguousarray(np.asarray(result).transpose(1, 0, 2)).reshape(B, S, H)
```

```python
from contextlib import ExitStack
from math import erf, exp, pi

import concourse.bass as bass
from concourse import mybir

P = 128
ALU = mybir.AluOpType
ACT = mybir.ActivationFunctionType
AX = mybir.AxisListType
F32 = mybir.dt.float32
F32R = mybir.dt.float32r
U32 = mybir.dt.uint32
I32 = mybir.dt.int32

TOP_K_RATIO = 0.3
HEADS = 4
LN_EPS = 1e-5
REPLACED = -3.0e38
ROUNDS = 3
GUESS_SHARE = 0.985
DAMPING = 0.9
EARLY = 2
B2_AFTER = 1
LAG = 2


def normal_density(z):
    return exp(-z * z / 2) / (2 * pi) ** 0.5


def normal_quantile(share):
    low, high = -8.0, 8.0
    for _ in range(60):
        middle = (low + high) / 2
        if (1 + erf(middle / 2 ** 0.5)) / 2 < share:
            low = middle
        else:
            high = middle
    return low


def small_columns(experts, chunks):
    return [("gamma", 1), ("alpha", experts), ("gate_w", chunks * experts), ("b1", experts * chunks),
            ("identity", P), ("expert", experts), ("above", 8 * ROUNDS)]


def xattn_moe_program(nc, x, attn, small, w, b2, out):
    HID = x.shape[2]
    D = attn.shape[0]
    TOKENS = attn.shape[1] - 2 * D
    EXPERTS = w.shape[1]
    N = HID
    BATCHES = TOKENS // N
    TILES = N // P
    CH = HID // P
    STEPS = BATCHES * EXPERTS
    SIM_SCALE = 1.0 / ((D // HEADS) ** 0.5 * HEADS)
    TOP_K = max(1, int(N * TOP_K_RATIO))
    ALL_ROUNDS = (TOP_K + 7) // 8
    LAST = (TOP_K - 1) % 8
    WINDOW = 8 * ROUNDS
    MIDDLE = TOP_K - (WINDOW + 1) / 2
    Z = GUESS_SHARE * normal_quantile(1 - (MIDDLE + 0.5) / N)
    SIGMA = (pi / 2) ** 0.5 / N ** 2
    PER_COUNT = DAMPING * SIGMA / (N * normal_density(Z))

    with ExitStack() as ctx:
        def sb(name, shape, dt=F32):
            return ctx.enter_context(nc.sbuf_tensor(name, shape, dt))

        def bank(name):
            return ctx.enter_context(nc.psum_tensor(name, [P, 512], F32))

        def sem(name):
            return ctx.enter_context(nc.semaphore(name))

        attn_sb = sb("attn_sb", [D, 2 * D + TOKENS])
        wq_sb, wk_sb, ctx_sb = attn_sb[:, 0:D], attn_sb[:, D:2 * D], attn_sb[:, 2 * D:]
        x_sb = sb("x_sb", [P, BATCHES, TILES, HID])
        small_sb = sb("small_sb", [P, small.shape[1]])
        cut = {}
        at = 0
        for name, width in small_columns(EXPERTS, CH):
            cut[name] = small_sb[:, at:at + width]
            at += width
        gamma_sb, alpha_sb, ident_sb, iota_sb, above_sb = (
            cut[n] for n in ("gamma", "alpha", "identity", "expert", "above"))
        gate_sb = cut["gate_w"].rearrange("p (c e) -> p c e", c=CH)
        b1_sb = cut["b1"].rearrange("p (e c) -> p e c", c=CH)
        w_sb = sb("w_sb", [P, EXPERTS, 2, CH, HID])
        b2_sb = sb("b2_sb", [EXPERTS, HID])
        gate_hi = sb("gate_hi", [P, CH, EXPERTS], F32R)
        gate_lo = sb("gate_lo", [P, CH, EXPERTS], F32R)
        w_hi = sb("w_hi", [P, EXPERTS, 2, CH, HID], F32R)
        w_lo = sb("w_lo", [P, EXPERTS, 2, CH, HID], F32R)
        m_sb = sb("m_sb", [D, D])
        u_sb = sb("u_sb", [D, TOKENS])
        sim = sb("sim", [P, BATCHES, TILES, N])
        act_waste = sb("act_waste", [P, TILES, N])
        row_sum = sb("row_sum", [P, BATCHES, TILES])
        spread = sb("spread", [P, BATCHES, TILES])
        neg_mean = sb("neg_mean", [P, TILES])
        neg_guess = sb("neg_guess", [P, BATCHES, TILES])
        signs = sb("signs", [P, BATCHES, TILES])
        off = sb("off", [P, TILES])
        guess = sb("guess", [P, TILES])
        above = sb("above", [P, TILES, N])
        count = sb("count", [P, TILES])
        few = sb("few", [P, TILES])
        missed = sb("missed", [P, TILES])
        ones = sb("ones", [P, 1])
        any_missed = sb("any_missed", [1, BATCHES])
        left = sb("left", [P, TILES, N])
        top = sb("top", [P, TILES, WINDOW])
        top8 = sb("top8", [P, TILES, 8])
        chosen = sb("chosen", [P, TILES, WINDOW])
        threshold = sb("threshold", [P, TILES])
        half = sb("half", [P, BATCHES, TILES, N])
        gam = sb("gam", [P, 4])
        stats = sb("stats", [P, TILES, 6])
        mv1 = sb("mv1", [P, BATCHES, TILES, 2])
        veps1 = sb("veps1", [P, BATCHES, TILES])
        rstd1 = sb("rstd1", [P, BATCHES, TILES])
        mul1 = sb("mul1", [P, BATCHES, TILES])
        add1 = sb("add1", [P, BATCHES, TILES])
        stats2 = sb("stats2", [P, TILES, 6])
        mv2 = sb("mv2", [P, BATCHES, TILES, 2])
        veps2 = sb("veps2", [P, BATCHES, TILES])
        rstd2 = sb("rstd2", [P, BATCHES, TILES])
        neg_half = sb("neg_half", [P, TILES])
        x1 = sb("x1", [P, BATCHES, TILES, HID])
        xn = sb("xn", [P, TILES, HID])
        xt_hi = sb("xt_hi", [P, 2, CH, N], F32R)
        xt_lo = sb("xt_lo", [P, 2, CH, N], F32R)
        logits = sb("logits", [P, TILES, EXPERTS])
        best = sb("best", [P, TILES, 8])
        best_at = sb("best_at", [P, TILES, 8], U32)
        best_f = sb("best_f", [P, TILES, 2])
        gap = sb("gap", [P, TILES])
        gap_th = sb("gap_th", [P, TILES])
        score = sb("score", [P, 2, TILES])
        pick = sb("pick", [P, 2, TILES, EXPERTS])
        comb = sb("comb", [P, BATCHES, TILES, EXPERTS])
        comb_t = sb("comb_t", [EXPERTS, TILES, P])
        h_act = sb("h_act", [P, 2, CH, N])
        h_hi = sb("h_hi", [P, LAG + 1, CH, N], F32R)
        h_lo = sb("h_lo", [P, LAG + 1, CH, N], F32R)
        acc = sb("acc", [P, 2, TILES, HID])

        p_h = [bank("p_h0"), bank("p_h1")]
        p_y = [bank("p_y0"), bank("p_y1")]
        p_s = bank("p_s")
        p_a = bank("p_a")
        p_x = bank("p_x")
        p_g = bank("p_g")

        def tiled(b):
            return b[:, :].rearrange("p (t n) -> p t n", t=TILES)

        attn_in = sem("attn_in")
        ctx_in = sem("ctx_in")
        x_in = [sem("x_in0"), sem("x_in_rest")]
        small_in = sem("small_in")
        b2_in = sem("b2_in")
        w_in = [sem(f"w_in{e}") for e in range(EXPERTS)]
        out_done = [sem(f"out_done{b}") for b in range(BATCHES)]
        m_ready = sem("m_ready")
        m_copied = sem("m_copied")
        u_ready = sem("u_ready")
        u_copied = sem("u_copied")
        sim_ready = sem("sim_ready")
        sim_copied = sem("sim_copied")
        gam_th = sem("gam_th")
        gam_ready = sem("gam_ready")
        sig_th = sem("sig_th")
        sig_ready = sem("sig_ready")
        spread_ready = sem("spread_ready")
        mean_ready = sem("mean_ready")
        guess_ready = sem("guess_ready")
        signs_ready = sem("signs_ready")
        off_ready = sem("off_ready")
        counted = sem("counted")
        missed_ready = sem("missed_ready")
        missed_sum = sem("missed_sum")
        missed_known = sem("missed_known")
        search = sem("search")
        search_all = [sem(f"search_all{b}") for b in range(BATCHES)]
        chosen_ready = sem("chosen_ready")
        masked = sem("masked")
        masked_t = sem("masked_t")
        ln1_stats = sem("ln1_stats")
        ln1_agg = sem("ln1_agg")
        better_ready = sem("better_ready")
        few_ready = sem("few_ready")
        b2_added = sem("b2_added")
        ln1_veps = sem("ln1_veps")
        ln1_rstd = sem("ln1_rstd")
        ln1_mul = sem("ln1_mul")
        base_ready = sem("base_ready")
        base_sum = sem("base_sum")
        x1_ready = sem("x1_ready")
        ln2_stats = sem("ln2_stats")
        ln2_agg = sem("ln2_agg")
        ln2_veps = sem("ln2_veps")
        ln2_rstd = sem("ln2_rstd")
        xn_ready = sem("xn_ready")
        xn_t = sem("xn_t")
        xt_hi_ready = sem("xt_hi_ready")
        xt_lo_ready = sem("xt_lo_ready")
        gate_hi_ready = sem("gate_hi_ready")
        gate_lo_ready = sem("gate_lo_ready")
        logits_ready = sem("logits_ready")
        gating = sem("gating")
        gap_ready = sem("gap_ready")
        gap_th_ready = sem("gap_th_ready")
        comb_ready = sem("comb_ready")
        comb_tr = sem("comb_tr")
        comb_t_ready = sem("comb_t_ready")
        b2_ready = sem("b2_ready")
        const_set = sem("const_set")
        w_hi_ready = sem("w_hi_ready")
        w_lo_ready = sem("w_lo_ready")
        w_lo_early = sem("w_lo_early")
        h_ready = sem("h_ready")
        h_act_ready = sem("h_act_ready")
        h_hi_ready = sem("h_hi_ready")
        h_lo_ready = sem("h_lo_ready")
        y_ready = sem("y_ready")
        y_added = sem("y_added")

        block = ctx.enter_context(nc.Block())

        U_BANKS = (p_a, p_x, p_y[0], p_y[1])
        SIM_BANKS = ((p_s, p_h[0]), (p_h[1],) * TILES, (p_g,) * TILES, (p_s,) * TILES)

        @block.sync
        def _(sp):
            first = 2 * D + N
            sp.dma_start(attn_sb[:, 0:first], attn[:, 0:first]).then_inc(attn_in, 16)
            sp.dma_start(small_sb[:], small).then_inc(small_in, 16)
            sp.dma_start(x_sb[:, 0], x[:, 0:TILES]).then_inc(x_in[0], 16)
            sp.dma_start(w_sb[:, 0], w[:, 0]).then_inc(w_in[0], 16)
            sp.dma_start(attn_sb[:, first:], attn[:, first:]).then_inc(ctx_in, 16)
            for e in range(1, EXPERTS):
                sp.dma_start(w_sb[:, e], w[:, e]).then_inc(w_in[e], 16)
                if e == 1:
                    sp.dma_start(b2_sb[:], b2).then_inc(b2_in, 16)
                if e == 3:
                    sp.dma_start(x_sb[:, 1:].rearrange("p b t n -> p (b t) n"), x[:, TILES:]).then_inc(x_in[1], 16)
            for b in range(BATCHES):
                sp.wait_ge(y_added, (b + 1) * EXPERTS)
                sp.dma_start(out[:, b * TILES:(b + 1) * TILES], acc[:, b % 2]).then_inc(out_done[b], 16)
            for b in range(BATCHES):
                sp.wait_ge(out_done[b], 16)

        @block.tensor
        def _(pe):
            def u_of(b):
                nc.tensor.matmul(U_BANKS[b][0:D, 0:N], m_sb[:], ctx_sb[:, b * N:(b + 1) * N], start=True,
                                 stop=True).then_inc(u_ready, 1)

            def sim_of(b):
                pe.wait_ge(u_copied, b + 1)
                if b == BATCHES - 1:
                    pe.wait_ge(sim_copied, 1)
                for t in range(TILES):
                    n0 = b * N + t * P
                    nc.tensor.matmul(tiled(SIM_BANKS[b][t])[:, t, :], u_sb[:, n0:n0 + P],
                                     ctx_sb[:, b * N:(b + 1) * N], start=True, stop=True).then_inc(sim_ready, 1)

            def similarities():
                pe.wait_ge(attn_in, 16)
                nc.tensor.matmul(p_g[0:D, 0:D], wq_sb, wk_sb, start=True, stop=True).then_inc(m_ready, 1)
                pe.wait_ge(m_copied, 1)
                u_of(0)
                sim_of(0)
                pe.wait_ge(ctx_in, 16)
                for b in range(1, BATCHES):
                    u_of(b)
                for b in range(1, BATCHES):
                    sim_of(b)

            def sum_missed(b):
                pe.wait_ge(missed_ready, b + 1)
                if b == 0:
                    pe.wait_ge(u_copied, BATCHES)
                else:
                    pe.wait_ge(x1_ready, b)
                nc.tensor.matmul(p_a[0:1, 0:TILES], ones[:], missed[:], start=True, stop=True).then_inc(missed_sum, 1)

            def transpose_masked(b):
                pe.wait_ge(masked, b + 1)
                for t in range(TILES):
                    for r in range(TILES):
                        last = nc.tensor.transpose(tiled(p_a)[:, t, r * P:(r + 1) * P],
                                                   half[:, b, r, t * P:(t + 1) * P], ident_sb)
                last.then_inc(masked_t, 1)

            def transpose_xn(b):
                pe.wait_ge(xn_ready, b + 1)
                if b >= 1:
                    pe.wait_ge(xt_lo_ready, b)
                for k in range(CH):
                    for t in range(TILES):
                        last = nc.tensor.transpose(tiled(p_x)[:, k, t * P:(t + 1) * P],
                                                   xn[:, t, k * P:(k + 1) * P], ident_sb)
                last.then_inc(xn_t, 1)

            def gate(b):
                if b == 0:
                    pe.wait_ge(gate_lo_ready, 1)
                else:
                    pe.wait_ge(comb_t_ready, b)
                for t in range(TILES):
                    dst = p_g[:, t * EXPERTS:(t + 1) * EXPERTS]
                    trio = [(v, g, k) for v, g in ((xt_hi, gate_hi), (xt_hi, gate_lo), (xt_lo, gate_hi))
                            for k in range(CH)]
                    for n, (v, g, k) in enumerate(trio):
                        last = nc.tensor.matmul(dst, v[:, b % 2, k, t * P:(t + 1) * P], g[:, k, :],
                                                start=n == 0, stop=n == len(trio) - 1)
                last.then_inc(logits_ready, 1)

            def transpose_comb(b):
                pe.wait_ge(comb_ready, b + 1)
                for t in range(TILES):
                    last = nc.tensor.transpose(p_g[0:EXPERTS, 64 + t * P:64 + (t + 1) * P], comb[:, b, t, :],
                                               ident_sb)
                last.then_inc(comb_tr, 1)

            def bias_sums(b):
                pe.wait_ge(comb_t_ready, b + 1)
                if b == 0:
                    pe.wait_ge(b2_in, 16)
                else:
                    pe.wait_ge(b2_added, b)
                for t in range(TILES):
                    last = nc.tensor.matmul(tiled(p_s)[:, t, :], comb_t[:, t, :], b2_sb[:], start=True, stop=True)
                last.then_inc(b2_ready, 1)

            def up(s):
                b, e = divmod(s, EXPERTS)
                if b == 0:
                    wait_for_weights(e)
                if s >= 2:
                    pe.wait_ge(h_act_ready, s - 1)
                else:
                    pe.wait_ge(sim_copied, BATCHES * TILES)
                for c in range(CH):
                    dst = tiled(p_h[s % 2])[:, c, :]
                    trio = [(w_, v, k) for w_, v in ((w_hi, xt_hi), (w_lo, xt_hi), (w_hi, xt_lo)) for k in range(CH)]
                    for n, (w_, v, k) in enumerate(trio):
                        last = nc.tensor.matmul(dst, w_[:, e, 0, k, c * P:(c + 1) * P], v[:, b % 2, k, :],
                                                start=n == 0, stop=n == len(trio) - 1)
                last.then_inc(h_ready, 1)

            def wait_for_weights(e):
                if e < EARLY:
                    pe.wait_ge(w_lo_early, e + 1)
                else:
                    pe.wait_ge(w_lo_ready, e - EARLY + 1)

            def down(s):
                b, e = divmod(s, EXPERTS)
                pe.wait_ge(h_lo_ready, s + 1)
                if s >= 2:
                    pe.wait_ge(y_added, s - 1)
                for t in range(TILES):
                    dst = tiled(p_y[s % 2])[:, t, :]
                    trio = [(v, w_, k) for v, w_ in ((h_hi, w_hi), (h_hi, w_lo), (h_lo, w_hi)) for k in range(CH)]
                    for n, (v, w_, k) in enumerate(trio):
                        last = nc.tensor.matmul(dst, v[:, s % (LAG + 1), k, t * P:(t + 1) * P], w_[:, e, 1, k, :],
                                                start=n == 0, stop=n == len(trio) - 1)
                last.then_inc(y_ready, 1)

            similarities()
            sum_missed(0)
            transpose_masked(0)
            transpose_xn(0)
            for s in range(STEPS + LAG):
                b, e = divmod(s, EXPERTS)
                more = b + 1 < BATCHES
                if s < STEPS:
                    if e == 0:
                        pe.wait_ge(xt_lo_ready, b + 1)
                        gate(b)
                    up(s)
                    if e == 2:
                        transpose_comb(b)
                    if e == 3:
                        bias_sums(b)
                if more and e == 3:
                    sum_missed(b + 1)
                if more and e == 5:
                    transpose_masked(b + 1)
                if more and e == 7:
                    transpose_xn(b + 1)
                if s >= LAG:
                    down(s - LAG)

        @block.scalar
        def _(act):
            def u_copy(b):
                act.wait_ge(u_ready, b + 1)
                nc.scalar.activation(u_sb[:, b * N:(b + 1) * N], U_BANKS[b][0:D, 0:N], ACT.Copy,
                                     scale=SIM_SCALE).then_inc(u_copied, 1)

            def sim_copy(b):
                for t in range(TILES):
                    act.wait_ge(sim_ready, 1 + t if b == 0 else (b + 1) * TILES)
                    nc.scalar.activation(sim[:, b, t], tiled(SIM_BANKS[b][t])[:, t, :], ACT.Copy,
                                         accum_out=row_sum[:, b, t:t + 1]).then_inc(sim_copied, 1)

            def spread_of(b):
                act.wait_ge(sim_copied, (b + 1) * TILES)
                for t in range(TILES):
                    last = nc.scalar.activation(act_waste[:, t], sim[:, b, t], ACT.Abs, scale=-float(N),
                                                bias=row_sum[:, b, t:t + 1], accum_out=spread[:, b, t:t + 1])
                last.then_inc(spread_ready, 1)

            def signs_of(b):
                act.wait_ge(guess_ready, b + 1)
                for t in range(TILES):
                    last = nc.scalar.activation(act_waste[:, t], sim[:, b, t], ACT.Sign,
                                                bias=neg_guess[:, b, t:t + 1], accum_out=signs[:, b, t:t + 1])
                last.then_inc(signs_ready, 1)

            def sigmoid(b):
                nc.scalar.activation(half[:, b], sim[:, b], ACT.Tanh, scale=0.5).then_inc(sig_th, 1)
                act.wait_ge(sig_th, b + 1)
                if b == 0:
                    act.wait_ge(gam_ready, 1)
                nc.scalar.activation(half[:, b], half[:, b], ACT.Identity, scale=gam[:, 1:2],
                                     bias=gam[:, 1:2]).then_inc(sig_ready, 1)

            def weight_hi(e):
                act.wait_ge(w_in[e], 16)
                nc.scalar.activation(w_hi[:, e], w_sb[:, e], ACT.Copy).then_inc(w_hi_ready, 1)

            def xt_hi_of(b):
                act.wait_ge(xn_t, b + 1)
                if b >= 2:
                    act.wait_ge(h_ready, (b - 1) * EXPERTS)
                nc.scalar.activation(xt_hi[:, b % 2], tiled(p_x), ACT.Copy).then_inc(xt_hi_ready, 1)

            def gelu(s):
                b, e = divmod(s, EXPERTS)
                act.wait_ge(h_ready, s + 1)
                if s >= 2:
                    act.wait_ge(h_lo_ready, s - 1)
                for c in range(CH):
                    last = nc.scalar.activation(h_act[:, s % 2, c], tiled(p_h[s % 2])[:, c, :], ACT.Gelu,
                                                bias=b1_sb[:, e, c:c + 1])
                last.then_inc(h_act_ready, 1)

            def hidden_hi(s):
                act.wait_ge(h_act_ready, s + 1)
                if s > LAG:
                    act.wait_ge(y_ready, s - LAG)
                nc.scalar.activation(h_hi[:, s % (LAG + 1)], h_act[:, s % 2], ACT.Copy).then_inc(h_hi_ready, 1)

            def comb_copy(b):
                act.wait_ge(comb_tr, b + 1)
                nc.scalar.activation(comb_t[:], p_g[0:EXPERTS, 64:64 + N].rearrange("e (t p) -> e t p", t=TILES),
                                     ACT.Copy).then_inc(comb_t_ready, 1)

            nc.scalar.preload_act_table(ACT.Gelu)
            act.wait_ge(m_ready, 1)
            nc.scalar.activation(m_sb[:], p_g[0:D, 0:D], ACT.Copy).then_inc(m_copied, 1)
            u_copy(0)
            act.wait_ge(small_in, 16)
            nc.scalar.activation(gam[:, 0:1], gamma_sb, ACT.Tanh, scale=0.5).then_inc(gam_th, 1)
            sim_copy(0)
            spread_of(0)
            for b in range(1, BATCHES):
                u_copy(b)
            signs_of(0)
            weight_hi(0)
            sigmoid(0)
            nc.scalar.activation(gate_hi[:], gate_sb, ACT.Copy).then_inc(gate_hi_ready, 1)
            for b in range(1, BATCHES):
                sim_copy(b)
            for e in range(1, EXPERTS - 2):
                weight_hi(e)
            xt_hi_of(0)
            weight_hi(EXPERTS - 2)
            weight_hi(EXPERTS - 1)
            for s in range(STEPS):
                b, e = divmod(s, EXPERTS)
                more = b + 1 < BATCHES
                gelu(s)
                hidden_hi(s)
                if e == 0:
                    act.wait_ge(gap_ready, b + 1)
                    nc.scalar.activation(gap_th[:], gap[:], ACT.Tanh, scale=0.5).then_inc(gap_th_ready, 1)
                    if more:
                        spread_of(b + 1)
                if e == 1 and more:
                    signs_of(b + 1)
                if e == 2:
                    comb_copy(b)
                if e == 3 and more:
                    sigmoid(b + 1)
                if e == 7 and more:
                    xt_hi_of(b + 1)

        @block.gpsimd
        def _(pool):
            def rstd(veps, rs, b, veps_ready, ready):
                pool.wait_ge(veps_ready, b + 1)
                nc.gpsimd.tensor_tensor(rs[:, b, :], veps[:, b, :], neg_half[:], ALU.pow).then_inc(ready, 1)

            def weight_lo(e):
                pool.wait_ge(w_hi_ready, e + 1)
                nc.gpsimd.tensor_tensor(w_lo[:, e], w_sb[:, e], w_hi[:, e], ALU.subtract).then_inc(w_lo_ready, 1)

            def base(b):
                pool.wait_ge(ln1_mul, b + 1)
                for t in range(TILES):
                    last = nc.gpsimd.tensor_scalar(x_sb[:, b, t], x_sb[:, b, t], mul1[:, b, t:t + 1],
                                                   add1[:, b, t:t + 1], ALU.mult, ALU.add)
                last.then_inc(base_ready, 1)

            def add_masked(b):
                pool.wait_ge(masked, b + 1)
                pool.wait_ge(base_ready, b + 1)
                nc.gpsimd.tensor_tensor(x_sb[:, b], x_sb[:, b], half[:, b], ALU.add).then_inc(base_sum, 1)

            def hidden_lo(s):
                pool.wait_ge(h_hi_ready, s + 1)
                if s > LAG:
                    pool.wait_ge(y_ready, s - LAG)
                nc.gpsimd.tensor_tensor(h_lo[:, s % (LAG + 1)], h_act[:, s % 2], h_hi[:, s % (LAG + 1)],
                                        ALU.subtract).then_inc(h_lo_ready, 1)

            nc.gpsimd.memset(neg_half[:], -0.5).then_inc(const_set, 1)
            nc.gpsimd.memset(ones[:], 1.0).then_inc(const_set, 1)
            pool.wait_ge(const_set, 2)
            rstd(veps1, rstd1, 0, ln1_veps, ln1_rstd)
            pool.wait_ge(gate_hi_ready, 1)
            nc.gpsimd.tensor_tensor(gate_lo[:], gate_sb, gate_hi[:], ALU.subtract).then_inc(gate_lo_ready, 1)
            base(0)
            add_masked(0)
            rstd(veps2, rstd2, 0, ln2_veps, ln2_rstd)
            for e in range(EARLY, EARLY + 2):
                weight_lo(e)
            for s in range(STEPS):
                b, e = divmod(s, EXPERTS)
                more = b + 1 < BATCHES
                if b == 0 and EARLY + 2 + e < EXPERTS:
                    weight_lo(EARLY + 2 + e)
                hidden_lo(s)
                if more and e == 1:
                    rstd(veps1, rstd1, b + 1, ln1_veps, ln1_rstd)
                if more and e == 3:
                    base(b + 1)
                if more and e == 4:
                    add_masked(b + 1)
                if more and e == 6:
                    rstd(veps2, rstd2, b + 1, ln2_veps, ln2_rstd)

        @block.vector
        def _(dve):
            def moments(rows, stats_, mv, veps, stats_ready, agg_ready, veps_ready, b):
                for t in range(TILES):
                    last = nc.vector.bn_stats(stats_[:, t, :], rows[:, b, t])
                last.then_inc(stats_ready, 1)
                dve.wait_ge(stats_ready, b + 1)
                for t in range(TILES):
                    last = nc.vector.bn_aggr(mv[:, b, t, :], stats_[:, t, :])
                last.then_inc(agg_ready, 1)
                dve.wait_ge(agg_ready, b + 1)
                nc.vector.tensor_scalar(veps[:, b, :], mv[:, b, :, 1], LN_EPS, None, ALU.add).then_inc(veps_ready, 1)

            def ln1(b):
                dve.wait_ge(x_in[min(b, 1)], 16)
                moments(x_sb, stats, mv1, veps1, ln1_stats, ln1_agg, ln1_veps, b)

            def ln1_affine(b):
                dve.wait_ge(ln1_rstd, b + 1)
                nc.vector.tensor_scalar(mul1[:, b, :], rstd1[:, b, :], gam[:, 2:3], 1.0, ALU.mult, ALU.add)
                nc.vector.scalar_tensor_tensor(add1[:, b, :], mv1[:, b, :, 0], gam[:, 3:4], rstd1[:, b, :], ALU.mult,
                                               ALU.mult).then_inc(ln1_mul, 1)

            def gamma_terms():
                dve.wait_ge(gam_th, 1)
                nc.vector.tensor_scalar(gam[:, 1:2], gam[:, 0:1], 0.125, 0.125, ALU.mult, ALU.add)
                nc.vector.tensor_scalar(gam[:, 2:3], gam[:, 0:1], -0.5, 0.5, ALU.mult, ALU.add)
                nc.vector.tensor_scalar(gam[:, 3:4], gam[:, 0:1], 0.5, -0.5, ALU.mult, ALU.add).then_inc(gam_ready, 1)
                dve.wait_ge(gam_ready, 1)

            def weight_lo(e):
                dve.wait_ge(w_hi_ready, e + 1)
                nc.vector.tensor_tensor(w_lo[:, e], w_sb[:, e], w_hi[:, e], ALU.subtract).then_inc(w_lo_early, 1)

            def first_guess(b):
                nc.vector.tensor_scalar(neg_mean[:], row_sum[:, b, :], -1.0 / N, None, ALU.mult).then_inc(mean_ready, 1)
                dve.wait_ge(mean_ready, b + 1)
                nc.vector.scalar_tensor_tensor(neg_guess[:, b, :], spread[:, b, :], -Z * SIGMA, neg_mean[:], ALU.mult,
                                               ALU.add).then_inc(guess_ready, 1)

            def better_guess(b):
                dve.wait_ge(signs_ready, b + 1)
                nc.vector.tensor_scalar(off[:], signs[:, b, :], PER_COUNT / 2, PER_COUNT * (N / 2 - MIDDLE), ALU.mult,
                                        ALU.add).then_inc(off_ready, 1)
                dve.wait_ge(off_ready, 2 * b + 1)
                nc.vector.tensor_tensor(off[:], off[:], spread[:, b, :], ALU.mult).then_inc(off_ready, 1)
                dve.wait_ge(off_ready, 2 * b + 2)
                nc.vector.tensor_tensor(guess[:], off[:], neg_guess[:, b, :], ALU.subtract).then_inc(better_ready, 1)

            def count_above(b):
                dve.wait_ge(better_ready, b + 1)
                for t in range(TILES):
                    nc.vector.tensor_scalar(above[:, t], sim[:, b, t], guess[:, t:t + 1], None, ALU.is_ge, ALU.add,
                                            accum_out=count[:, t:t + 1]).then_inc(counted, 1)

            def flag_missed(b):
                dve.wait_ge(counted, (b + 1) * TILES)
                nc.vector.tensor_scalar(few[:], count[:], TOP_K - WINDOW, None, ALU.is_lt).then_inc(few_ready, 1)
                dve.wait_ge(few_ready, b + 1)
                if b:
                    dve.wait_ge(missed_sum, b)
                nc.vector.scalar_tensor_tensor(missed[:], count[:], TOP_K, few[:], ALU.is_ge, ALU.add).then_inc(
                    missed_ready, 1)

            steps = [0]

            def step_of_tile(ins):
                steps[0] += 1
                ins.then_inc(search, 1)

            def tile_before():
                dve.wait_ge(search, steps[0] - TILES + 1)

            def drop_above(b):
                for t in range(TILES):
                    dve.wait_ge(counted, b * TILES + t + 1)
                    step_of_tile(nc.vector.scalar_tensor_tensor(left[:, t], above[:, t], REPLACED, sim[:, b, t],
                                                                ALU.mult, ALU.add))

            def take_eight(r):
                for t in range(TILES):
                    tile_before()
                    step_of_tile(nc.vector.max(top[:, t, 8 * r:8 * r + 8], left[:, t]))

            def drop_eight(r):
                for t in range(TILES):
                    tile_before()
                    step_of_tile(nc.vector.match_replace(left[:, t], top[:, t, 8 * r:8 * r + 8], left[:, t], REPLACED))

            def choose(b):
                dve.wait_ge(search, steps[0])
                for t in range(TILES):
                    last = nc.vector.scalar_tensor_tensor(chosen[:, t], above_sb, count[:, t:t + 1], top[:, t, :],
                                                          ALU.is_equal, ALU.mult, accum_out=threshold[:, t:t + 1])
                last.then_inc(chosen_ready, 1)
                dve.wait_ge(chosen_ready, b + 1)

            def know_missed(b):
                dve.wait_ge(missed_sum, b + 1)
                nc.vector.tensor_reduce(any_missed[:, b:b + 1], p_a[0:1, 0:TILES], AX.X, ALU.add).then_inc(
                    missed_known, 1)

            def search_everything(b):
                n = 0
                for r in range(ALL_ROUNDS):
                    for t in range(TILES):
                        if n >= TILES:
                            dve.wait_ge(search_all[b], n - TILES + 1)
                        nc.vector.max(top8[:, t], sim[:, b, t] if r == 0 else left[:, t]).then_inc(search_all[b], 1)
                        n += 1
                    for t in range(TILES):
                        dve.wait_ge(search_all[b], n - TILES + 1)
                        if r < ALL_ROUNDS - 1:
                            nc.vector.match_replace(left[:, t], top8[:, t], sim[:, b, t] if r == 0 else left[:, t],
                                                    REPLACED).then_inc(search_all[b], 1)
                        else:
                            nc.vector.tensor_copy(threshold[:, t:t + 1], top8[:, t, LAST:LAST + 1]).then_inc(
                                search_all[b], 1)
                        n += 1
                dve.wait_ge(search_all[b], n)

            def search_again_if_missed(b):
                dve.wait_ge(missed_known, b + 1)
                rows = nc.vector.value_load(any_missed[0:1, b:b + 1].bitcast(I32))
                with nc.vector.If(rows > 0):
                    search_everything(b)

            def mask(b):
                dve.wait_ge(sig_ready, b + 1)
                for t in range(TILES):
                    last = nc.vector.scalar_tensor_tensor(half[:, b, t], sim[:, b, t], threshold[:, t:t + 1],
                                                          half[:, b, t], ALU.is_ge, ALU.mult)
                last.then_inc(masked, 1)

            def residual(b):
                dve.wait_ge(masked_t, b + 1)
                dve.wait_ge(base_sum, b + 1)
                nc.vector.tensor_tensor(x1[:, b], x_sb[:, b], tiled(p_a), ALU.add).then_inc(x1_ready, 1)
                dve.wait_ge(x1_ready, b + 1)
                moments(x1, stats2, mv2, veps2, ln2_stats, ln2_agg, ln2_veps, b)

            def normalise(b):
                dve.wait_ge(ln2_rstd, b + 1)
                if b:
                    dve.wait_ge(xn_t, b)
                for t in range(TILES):
                    last = nc.vector.tensor_scalar(xn[:, t], x1[:, b, t], mv2[:, b, t, 0:1], rstd2[:, b, t:t + 1],
                                                   ALU.subtract, ALU.mult)
                last.then_inc(xn_ready, 1)

            def xt_lo_of(b):
                dve.wait_ge(xt_hi_ready, b + 1)
                nc.vector.tensor_tensor(xt_lo[:, b % 2], tiled(p_x), xt_hi[:, b % 2], ALU.subtract).then_inc(
                    xt_lo_ready, 1)

            gated = [0]

            def step(ins):
                gated[0] += 1
                ins.then_inc(gating, 1)

            def settle():
                dve.wait_ge(gating, gated[0])

            def top2(b):
                dve.wait_ge(logits_ready, b + 1)
                step(nc.vector.tensor_copy(logits[:], p_g[:, 0:TILES * EXPERTS].rearrange("p (t e) -> p t e", t=TILES)))
                settle()
                for t in range(TILES):
                    step(nc.vector.max(best[:, t], logits[:, t]))
                settle()
                nc.vector.tensor_tensor(gap[:], best[:, :, 0], best[:, :, 1], ALU.subtract).then_inc(gap_ready, 1)
                for t in range(TILES):
                    step(nc.vector.max_index(best_at[:, t], best[:, t], logits[:, t]))
                settle()
                step(nc.vector.tensor_copy(best_f[:], best_at[:, :, 0:2]))

            def combine(b):
                dve.wait_ge(gap_th_ready, b + 1)
                step(nc.vector.tensor_scalar(score[:, 0], gap_th[:], 0.5, 0.5, ALU.mult, ALU.add))
                step(nc.vector.tensor_scalar(score[:, 1], gap_th[:], -0.5, 0.5, ALU.mult, ALU.add))
                settle()
                for j in range(2):
                    for t in range(TILES):
                        step(nc.vector.tensor_scalar(pick[:, j, t], iota_sb, best_f[:, t, j:j + 1],
                                                     score[:, j, t:t + 1], ALU.is_equal, ALU.mult))
                settle()
                step(nc.vector.tensor_tensor(pick[:, 0], pick[:, 0], pick[:, 1], ALU.add))
                settle()
                for t in range(TILES):
                    last = nc.vector.tensor_tensor(comb[:, b, t], pick[:, 0, t], alpha_sb, ALU.mult)
                last.then_inc(comb_ready, 1)
                dve.wait_ge(comb_ready, b + 1)

            def add_biases(b):
                dve.wait_ge(b2_ready, b + 1)
                dve.wait_ge(y_added, b * EXPERTS + B2_AFTER + 1)
                nc.vector.tensor_tensor(acc[:, b % 2], acc[:, b % 2], tiled(p_s), ALU.add).then_inc(b2_added, 1)

            def add_expert(s):
                b, e = divmod(s, EXPERTS)
                dve.wait_ge(y_ready, s + 1)
                if e:
                    dve.wait_ge(y_added, s)
                elif b >= 2:
                    dve.wait_ge(out_done[b - 2], 16)
                if e == B2_AFTER + 1:
                    dve.wait_ge(b2_added, b + 1)
                for t in range(TILES):
                    nc_in = acc[:, b % 2, t] if e else x1[:, b, t]
                    last = nc.vector.scalar_tensor_tensor(acc[:, b % 2, t], tiled(p_y[s % 2])[:, t, :],
                                                          comb[:, b, t, e:e + 1], nc_in, ALU.mult, ALU.add)
                last.then_inc(y_added, 1)

            ln1(0)
            gamma_terms()
            ln1_affine(0)
            dve.wait_ge(spread_ready, 1)
            first_guess(0)
            better_guess(0)
            count_above(0)
            flag_missed(0)
            drop_above(0)
            take_eight(0)
            drop_eight(0)
            take_eight(1)
            know_missed(0)
            drop_eight(1)
            take_eight(2)
            choose(0)
            search_again_if_missed(0)
            mask(0)
            weight_lo(0)
            residual(0)
            weight_lo(1)
            normalise(0)
            xt_lo_of(0)
            for s in range(STEPS + LAG):
                b, e = divmod(s, EXPERTS)
                nxt = b + 1
                if b < BATCHES and e == 0:
                    top2(b)
                    combine(b)
                if b < BATCHES and e == B2_AFTER + LAG + 1:
                    add_biases(b)
                if nxt < BATCHES:
                    if e == 1:
                        dve.wait_ge(spread_ready, nxt + 1)
                        first_guess(nxt)
                        ln1(nxt)
                    if e == 2:
                        better_guess(nxt)
                        count_above(nxt)
                        flag_missed(nxt)
                        drop_above(nxt)
                    if e == 3:
                        take_eight(0)
                        drop_eight(0)
                        take_eight(1)
                        ln1_affine(nxt)
                    if e == 4:
                        know_missed(nxt)
                        drop_eight(1)
                        take_eight(2)
                        choose(nxt)
                        search_again_if_missed(nxt)
                        mask(nxt)
                    if e == 6:
                        residual(nxt)
                    if e == 7:
                        normalise(nxt)
                        xt_lo_of(nxt)
                if s >= LAG:
                    add_expert(s - LAG)


def kernel(x, ctx_512, L0_xattn_Wq, L0_xattn_Wk, L0_xattn_gamma_raw, L0_ffn_gate_w, L0_ffn_fc1_w, L0_ffn_fc1_b,
           L0_ffn_fc2_w, L0_ffn_fc2_b, L0_ffn_alpha):
    import numpy as np
    import concourse.bacc as bacc
    from concourse.bass_utils import run_bass_kernel_spmd

    B, S, H = x.shape
    T = B * S // P
    E = L0_ffn_fc1_w.shape[0]
    C = H // P

    def rows(w):
        return np.asarray(w).reshape(E, C, P, -1).transpose(2, 0, 1, 3)

    def repeated(a):
        return np.broadcast_to(np.asarray(a, np.float32).reshape(1, -1), (P, np.size(a)))

    parts = {
        "gamma": repeated(L0_xattn_gamma_raw),
        "alpha": repeated(L0_ffn_alpha),
        "gate_w": np.asarray(L0_ffn_gate_w).reshape(C, P, E).transpose(1, 0, 2).reshape(P, -1),
        "b1": np.asarray(L0_ffn_fc1_b).reshape(E, C, P).transpose(2, 0, 1).reshape(P, -1),
        "identity": np.eye(P, dtype=np.float32),
        "expert": repeated(np.arange(E)),
        "above": repeated(max(1, int(S * TOP_K_RATIO)) - 1 - np.arange(8 * ROUNDS)),
    }
    arrays = {
        "x": np.asarray(x).reshape(T, P, H).transpose(1, 0, 2),
        "attn": np.concatenate([np.asarray(L0_xattn_Wq), np.asarray(L0_xattn_Wk),
                                np.asarray(ctx_512).reshape(B * S, -1).T], axis=1),
        "small": np.concatenate([parts[name] for name, _ in small_columns(E, C)], axis=1),
        "w": np.stack([rows(L0_ffn_fc1_w), rows(L0_ffn_fc2_w)], axis=2),
        "b2": np.asarray(L0_ffn_fc2_b),
    }
    arrays = {k: np.ascontiguousarray(v) for k, v in arrays.items()}
    nc = bacc.Bacc("TRN2", target_bir_lowering=False, num_devices=1)
    aps = {k: nc.dram_tensor(k, v.shape, mybir.dt.from_np(v.dtype), kind="ExternalInput").ap()
           for k, v in arrays.items()}
    out = nc.dram_tensor("out", (P, T, H), F32, kind="ExternalOutput").ap()
    xattn_moe_program(nc, out=out, **aps)
    result = run_bass_kernel_spmd(nc, [arrays], core_ids=[0]).results[0]["out"]
    return np.ascontiguousarray(np.asarray(result).transpose(1, 0, 2)).reshape(B, S, H)
```

```python
from contextlib import ExitStack
from math import erf, exp, pi

from concourse import mybir

P = 128
ALU = mybir.AluOpType
ACT = mybir.ActivationFunctionType
AX = mybir.AxisListType
F32 = mybir.dt.float32
F32R = mybir.dt.float32r
U32 = mybir.dt.uint32
I32 = mybir.dt.int32

TOP_K_RATIO = 0.3
HEADS = 4
LN_EPS = 1e-5
REPLACED = -3.0e38
ROUNDS = 3
DAMPING = 0.8
EARLY = 1
BEFORE_LN2 = 4
DVE_SPLITS = (6, 7)
B2_AFTER = 4
LAG = 2


def normal_density(z):
    return exp(-z * z / 2) / (2 * pi) ** 0.5


def normal_quantile(share):
    low, high = -8.0, 8.0
    for _ in range(60):
        middle = (low + high) / 2
        if (1 + erf(middle / 2 ** 0.5)) / 2 < share:
            low = middle
        else:
            high = middle
    return low


def small_columns(experts, chunks):
    return [("gamma", 1), ("alpha", experts), ("gate_w", chunks * experts), ("b1", experts * chunks),
            ("identity", P), ("expert", experts), ("above", 8 * ROUNDS), ("split", 2)]


def xattn_moe_program(nc, x, attn, small, w, b2, out):
    HID = x.shape[2]
    D = attn.shape[0]
    TOKENS = attn.shape[1] - 2 * D
    EXPERTS = w.shape[1]
    N = HID
    BATCHES = TOKENS // N
    TILES = N // P
    CH = HID // P
    STEPS = BATCHES * EXPERTS
    SIM_SCALE = 1.0 / ((D // HEADS) ** 0.5 * HEADS)
    TOP_K = max(1, int(N * TOP_K_RATIO))
    ALL_ROUNDS = (TOP_K + 7) // 8
    LAST = (TOP_K - 1) % 8
    WINDOW = 8 * ROUNDS
    MIDDLE = TOP_K - (WINDOW + 1) / 2
    Z = normal_quantile(1 - (MIDDLE + 0.5) / N)
    SIGMA = (pi / 2) ** 0.5 / N ** 2
    PER_COUNT = DAMPING * SIGMA / (N * normal_density(Z))

    with ExitStack() as ctx:
        def sb(name, shape, dt=F32):
            return ctx.enter_context(nc.sbuf_tensor(name, shape, dt))

        def bank(name):
            return ctx.enter_context(nc.psum_tensor(name, [P, 512], F32))

        def sem(name):
            return ctx.enter_context(nc.semaphore(name))

        attn_sb = sb("attn_sb", [D, 2 * D + TOKENS])
        wq_sb, wk_sb, ctx_sb = attn_sb[:, 0:D], attn_sb[:, D:2 * D], attn_sb[:, 2 * D:]
        x_sb = sb("x_sb", [P, BATCHES, TILES, HID])
        small_sb = sb("small_sb", [P, small.shape[1]])
        cut = {}
        at = 0
        for name, width in small_columns(EXPERTS, CH):
            cut[name] = small_sb[:, at:at + width]
            at += width
        gamma_sb, alpha_sb, ident_sb, iota_sb, above_sb, split_sb = (
            cut[n] for n in ("gamma", "alpha", "identity", "expert", "above", "split"))
        gate_sb = cut["gate_w"].rearrange("p (c e) -> p c e", c=CH)
        b1_sb = cut["b1"].rearrange("p (e c) -> p e c", c=CH)
        w_sb = sb("w_sb", [P, EXPERTS, 2, CH, HID])
        PARTS = 3
        b2_sb = sb("b2_sb", [PARTS * EXPERTS, HID])
        b2_hi = sb("b2_hi", [PARTS * EXPERTS, HID], F32R)
        b2_parts = sb("b2_parts", [PARTS * EXPERTS, HID], F32R)
        gate_parts = sb("gate_parts", [P, CH, 2, EXPERTS], F32R)
        w_hi = sb("w_hi", [P, EXPERTS, 2, CH, HID], F32R)
        w_lo = sb("w_lo", [P, EXPERTS, 2, CH, HID], F32R)
        m_sb = sb("m_sb", [D, D])
        u_sb = sb("u_sb", [D, TOKENS])
        sim = sb("sim", [P, BATCHES, TILES, N])
        act_waste = sb("act_waste", [P, TILES, N])
        row_sum = sb("row_sum", [P, BATCHES, TILES])
        spread = sb("spread", [P, BATCHES, TILES])
        neg_mean = sb("neg_mean", [P, TILES])
        neg_guess = sb("neg_guess", [P, BATCHES, TILES])
        signs = sb("signs", [P, BATCHES, TILES])
        off = sb("off", [P, TILES])
        guess = sb("guess", [P, TILES])
        above = sb("above", [P, TILES, N])
        count = sb("count", [P, TILES])
        few = sb("few", [P, TILES])
        missed = sb("missed", [P, TILES])
        ones = sb("ones", [P, 1])
        any_missed = sb("any_missed", [1, BATCHES])
        left = sb("left", [P, TILES, N])
        top = sb("top", [P, TILES, WINDOW])
        top8 = sb("top8", [P, TILES, 8])
        chosen = sb("chosen", [P, TILES, WINDOW])
        threshold = sb("threshold", [P, TILES])
        half = sb("half", [P, BATCHES, TILES, N])
        gam = sb("gam", [P, 4])
        stats = sb("stats", [P, TILES, 6])
        mv1 = sb("mv1", [P, BATCHES, TILES, 2])
        veps1 = sb("veps1", [P, BATCHES, TILES])
        rstd1 = sb("rstd1", [P, BATCHES, TILES])
        mul1 = sb("mul1", [P, BATCHES, TILES])
        add1 = sb("add1", [P, BATCHES, TILES])
        stats2 = sb("stats2", [P, TILES, 6])
        mv2 = sb("mv2", [P, BATCHES, TILES, 2])
        veps2 = sb("veps2", [P, BATCHES, TILES])
        rstd2 = sb("rstd2", [P, BATCHES, TILES])
        neg_half = sb("neg_half", [P, TILES])
        x1 = sb("x1", [P, BATCHES, TILES, HID])
        xn = sb("xn", [P, TILES, HID])
        xt_hi = sb("xt_hi", [P, 2, CH, N], F32R)
        xt_lo = sb("xt_lo", [P, 2, CH, N], F32R)
        logits = sb("logits", [P, TILES, EXPERTS])
        logits_t = sb("logits_t", [2 * EXPERTS, N])
        best = sb("best", [P, TILES, 8])
        best_at = sb("best_at", [P, TILES, 8], U32)
        best_f = sb("best_f", [P, TILES, 2])
        gap = sb("gap", [P, TILES])
        gap_th = sb("gap_th", [P, TILES])
        score = sb("score", [P, TILES, 2])
        picked = sb("picked", [P, TILES, 2, EXPERTS])
        weight = sb("weight", [P, TILES, EXPERTS])
        comb = sb("comb", [P, BATCHES, TILES, PARTS, EXPERTS])
        comb_hi = sb("comb_hi", [PARTS * EXPERTS, N], F32R)
        comb_parts = sb("comb_parts", [PARTS * EXPERTS, N], F32R)
        h_act = sb("h_act", [P, 2, CH, N])
        h_hi = sb("h_hi", [P, LAG + 1, CH, N], F32R)
        h_lo = sb("h_lo", [P, LAG + 1, CH, N], F32R)
        acc = sb("acc", [P, 2, TILES, HID])

        p_h = [bank("p_h0"), bank("p_h1")]
        p_y = [bank("p_y0"), bank("p_y1")]
        p_s = bank("p_s")
        p_a = bank("p_a")
        p_x = bank("p_x")
        def y_bank(s, t):
            return p_s if s == STEPS - 1 and t == 1 else p_y[s % 2]

        XT_BANKS = (p_x, p_a)
        p_g = bank("p_g")

        def tiled(b):
            return b[:, :].rearrange("p (t n) -> p t n", t=TILES)

        attn_in = sem("attn_in")
        ctx_in = sem("ctx_in")
        x_in = [sem("x_in0"), sem("x_in_rest")]
        small_in = sem("small_in")
        b2_in = sem("b2_in")
        w_in = [sem(f"w_in{e}") for e in range(EXPERTS)]
        out_done = [sem(f"out_done{b}") for b in range(BATCHES)]
        m_ready = sem("m_ready")
        m_copied = sem("m_copied")
        u_ready = sem("u_ready")
        u_copied = sem("u_copied")
        u_mid_copied = sem("u_mid_copied")
        sim_ready = sem("sim_ready")
        sim_copied = sem("sim_copied")
        sim0_copied = sem("sim0_copied")
        gam_th = sem("gam_th")
        gam_ready = sem("gam_ready")
        sig_th = sem("sig_th")
        sig_ready = sem("sig_ready")
        spread_ready = sem("spread_ready")
        mean_ready = sem("mean_ready")
        guess_ready = sem("guess_ready")
        signs_ready = sem("signs_ready")
        off_ready = sem("off_ready")
        counted = sem("counted")
        missed_ready = sem("missed_ready")
        missed_sum = sem("missed_sum")
        missed_known = sem("missed_known")
        search = sem("search")
        search_all = [sem(f"search_all{b}") for b in range(BATCHES)]
        chosen_ready = sem("chosen_ready")
        masked = sem("masked")
        masked_t = sem("masked_t")
        ln1_stats = sem("ln1_stats")
        ln1_agg = sem("ln1_agg")
        better_ready = sem("better_ready")
        few_ready = sem("few_ready")
        b2_added = sem("b2_added")
        ln1_veps = sem("ln1_veps")
        ln1_rstd = sem("ln1_rstd")
        ln1_mul = sem("ln1_mul")
        base_ready = sem("base_ready")
        base_sum = sem("base_sum")
        x1_ready = sem("x1_ready")
        ln2_stats = sem("ln2_stats")
        ln2_agg = sem("ln2_agg")
        ln2_veps = sem("ln2_veps")
        ln2_rstd = sem("ln2_rstd")
        xn_ready = sem("xn_ready")
        xn_t = sem("xn_t")
        xt_hi_ready = sem("xt_hi_ready")
        xt_lo_ready = sem("xt_lo_ready")
        gate_hi_ready = sem("gate_hi_ready")
        gate_lo_ready = sem("gate_lo_ready")
        logits_t_ready = sem("logits_t_ready")
        logits_t_copied = sem("logits_t_copied")
        logits_ready = sem("logits_ready")
        gating = sem("gating")
        gap_ready = sem("gap_ready")
        gap_th_ready = sem("gap_th_ready")
        comb_ready = sem("comb_ready")
        comb_tr = sem("comb_tr")
        b2_hi_ready = sem("b2_hi_ready")
        b2_parts_ready = sem("b2_parts_ready")
        comb_hi_ready = sem("comb_hi_ready")
        comb_parts_ready = sem("comb_parts_ready")
        b2_ready = sem("b2_ready")
        const_set = sem("const_set")
        w_hi_early = sem("w_hi_early")
        w_hi_ready = sem("w_hi_ready")
        w_lo_ready = [[sem(f"w_lo_ready{e}_{j}") for j in range(2)] for e in range(EXPERTS)]
        h_ready = sem("h_ready")
        h_act_ready = sem("h_act_ready")
        h_hi_ready = sem("h_hi_ready")
        h_lo_ready = sem("h_lo_ready")
        h_lo_last = sem("h_lo_last")
        y_ready = sem("y_ready")
        y_added = sem("y_added")

        block = ctx.enter_context(nc.Block())

        COMB_T = p_g[0:PARTS * EXPERTS, 0:N]
        LOGITS_T = p_g[0:2 * EXPERTS, 0:N]
        LOGIT_PARTS = p_g[:, N:N + TILES * 2 * EXPERTS].rearrange("p (t j e) -> p t j e", t=TILES, j=2)
        U_BANKS = (p_a, p_x, p_y[0], p_y[1])
        SIM_BANKS = ((p_s, p_h[0]), (p_h[1],) * TILES, (p_g,) * TILES, (p_s,) * TILES)

        def sim_count(b, t):
            return 1 + (b - 1) * TILES + t + 1

        def wait_for_sim(engine, b, t):
            if b == 0 and t:
                engine.wait_ge(sim0_copied, TILES - 1)
            else:
                engine.wait_ge(sim_copied, sim_count(b, t) if b else 1)

        @block.sync
        def _(sp):
            first = 2 * D + N
            sp.dma_start(attn_sb[:, 0:first], attn[:, 0:first]).then_inc(attn_in, 16)
            sp.dma_start(small_sb[:], small).then_inc(small_in, 16)
            sp.dma_start(x_sb[:, 0], x[:, 0:TILES]).then_inc(x_in[0], 16)
            sp.dma_start(w_sb[:, 0], w[:, 0]).then_inc(w_in[0], 16)
            sp.dma_start(attn_sb[:, first:], attn[:, first:]).then_inc(ctx_in, 16)
            for e in range(1, EXPERTS):
                sp.dma_start(w_sb[:, e], w[:, e]).then_inc(w_in[e], 16)
                if e == 1:
                    sp.dma_start(b2_sb[:], b2).then_inc(b2_in, 16)
                if e == 3:
                    sp.dma_start(x_sb[:, 1:].rearrange("p b t n -> p (b t) n"), x[:, TILES:]).then_inc(x_in[1], 16)
            for b in range(BATCHES - 1):
                sp.wait_ge(y_added, (b + 1) * EXPERTS)
                sp.dma_start(out[:, b * TILES:(b + 1) * TILES], acc[:, b % 2]).then_inc(out_done[b], 16)
            for t in range(TILES):
                b = BATCHES - 1
                sp.wait_ge(y_added, STEPS + t)
                sp.dma_start(out[:, b * TILES + t], acc[:, b % 2, t]).then_inc(out_done[b], 16)
            for b in range(BATCHES):
                sp.wait_ge(out_done[b], 16 if b < BATCHES - 1 else 16 * TILES)

        @block.tensor
        def _(pe):
            def u_of(b):
                nc.tensor.matmul(U_BANKS[b][0:D, 0:N], m_sb[:], ctx_sb[:, b * N:(b + 1) * N], start=True,
                                 stop=True).then_inc(u_ready, 1)

            def sim_of(b):
                if b in (0, BATCHES - 1):
                    pe.wait_ge(u_copied, 1 if b == 0 else 2)
                else:
                    pe.wait_ge(u_mid_copied, b)
                if b == BATCHES - 1:
                    pe.wait_ge(sim_copied, 1)
                for t in range(TILES):
                    n0 = b * N + t * P
                    nc.tensor.matmul(tiled(SIM_BANKS[b][t])[:, t, :], u_sb[:, n0:n0 + P],
                                     ctx_sb[:, b * N:(b + 1) * N], start=True, stop=True).then_inc(sim_ready, 1)

            def sum_missed(b):
                pe.wait_ge(missed_ready, b + 1)
                if b == 0:
                    pe.wait_ge(u_copied, 1)
                else:
                    pe.wait_ge(xt_lo_ready, b * CH)
                nc.tensor.matmul(p_a[0:1, 0:TILES], ones[:], missed[:], start=True, stop=True).then_inc(missed_sum, 1)

            def similarities():
                pe.wait_ge(attn_in, 16)
                nc.tensor.matmul(p_g[0:D, 0:D], wq_sb, wk_sb, start=True, stop=True).then_inc(m_ready, 1)
                pe.wait_ge(m_copied, 1)
                u_of(0)
                sim_of(0)
                pe.wait_ge(ctx_in, 16)
                for b in range(1, BATCHES):
                    u_of(b)
                for b in range(1, BATCHES):
                    if b == BATCHES - 1:
                        sum_missed(0)
                    sim_of(b)

            def transpose_masked(b):
                for r in range(TILES):
                    pe.wait_ge(masked, b * TILES + r + 1)
                    for t in range(TILES):
                        last = nc.tensor.transpose(tiled(p_a)[:, t, r * P:(r + 1) * P],
                                                   half[:, b, r, t * P:(t + 1) * P], ident_sb)
                last.then_inc(masked_t, 1)

            def transpose_xn(b):
                pe.wait_ge(x1_ready, (b + 1) * TILES)
                if b:
                    pe.wait_ge(xt_lo_ready, b * CH)
                for t in range(TILES):
                    pe.wait_ge(xn_ready, b * TILES + t + 1)
                    for k in range(CH):
                        last = nc.tensor.transpose(XT_BANKS[k][:, t * P:(t + 1) * P],
                                                   xn[:, t, k * P:(k + 1) * P], ident_sb)
                        if t == TILES - 1:
                            last.then_inc(xn_t, 1)

            def gate(b):
                if b == 0:
                    pe.wait_ge(gate_lo_ready, 1)
                else:
                    pe.wait_ge(comb_parts_ready, b)
                for n, (v, k) in enumerate((v, k) for v in (xt_hi, xt_lo) for k in range(CH)):
                    last = nc.tensor.matmul(LOGITS_T, gate_parts[:, k].rearrange("p j e -> p (j e)"),
                                            v[:, b % 2, k, :], start=n == 0, stop=n == 2 * CH - 1)
                last.then_inc(logits_t_ready, 1)

            def turn_logits(b):
                pe.wait_ge(logits_t_copied, b + 1)
                for t in range(TILES):
                    last = nc.tensor.transpose(LOGIT_PARTS[:, t].rearrange("p j e -> p (j e)"),
                                               logits_t[:, t * P:(t + 1) * P],
                                               ident_sb[0:2 * EXPERTS, 0:2 * EXPERTS])
                last.then_inc(logits_ready, 1)

            def transpose_comb(b):
                pe.wait_ge(comb_ready, b + 1)
                for t in range(TILES):
                    last = nc.tensor.transpose(COMB_T[:, t * P:(t + 1) * P],
                                               comb[:, b, t].rearrange("p j e -> p (j e)"), ident_sb)
                last.then_inc(comb_tr, 1)

            def bias_sums(b):
                pe.wait_ge(comb_parts_ready, b + 1)
                if b == 0:
                    pe.wait_ge(b2_parts_ready, 1)
                else:
                    pe.wait_ge(b2_added, b)
                for t in range(TILES):
                    last = nc.tensor.matmul(tiled(p_s)[:, t, :], comb_parts[:, t * P:(t + 1) * P], b2_parts[:],
                                            start=True, stop=True)
                last.then_inc(b2_ready, 1)

            def keep_busy(products):
                pe.wait_ge(w_lo_ready[0][0], 1)
                pe.wait_ge(u_copied, 2)
                for _ in range(products):
                    nc.tensor.matmul(p_y[1][:, 0:N], w_hi[:, 0, 0, 0, 0:P], w_hi[:, 0, 0, 0, :], start=True, stop=True)

            def up(s):
                b, e = divmod(s, EXPERTS)
                if b == 0:
                    pe.wait_ge(w_lo_ready[e][0], 1)
                if s >= 2:
                    pe.wait_ge(h_act_ready, s - 1)
                else:
                    pe.wait_ge(sim_copied, sim_count(BATCHES - 1, TILES - 1))
                trio = [(w_, xt_hi, k) for k in range(CH) for w_ in (w_hi, w_lo)]
                trio += [(w_hi, xt_lo, k) for k in range(CH)]
                for c in range(CH):
                    dst = tiled(p_h[s % 2])[:, c, :]
                    for n, (w_, v, k) in enumerate(trio):
                        if e == 0 and c == 0 and w_ is w_hi:
                            pe.wait_ge(xt_hi_ready if v is xt_hi else xt_lo_ready, b * CH + k + 1)
                        last = nc.tensor.matmul(dst, w_[:, e, 0, k, c * P:(c + 1) * P], v[:, b % 2, k, :],
                                                start=n == 0, stop=n == len(trio) - 1)
                last.then_inc(h_ready, 1)

            def down(s):
                b, e = divmod(s, EXPERTS)
                if b == 0:
                    pe.wait_ge(w_lo_ready[e][1], 1)
                pe.wait_ge(h_hi_ready, s + 1)
                if s >= 2:
                    pe.wait_ge(y_added, s - 1)
                for t in range(TILES):
                    if s == STEPS - 1 and t == 1:
                        pe.wait_ge(b2_added, BATCHES)
                    dst = tiled(y_bank(s, t))[:, t, :]
                    trio = [(v, w_, k) for v, w_ in ((h_hi, w_hi), (h_hi, w_lo), (h_lo, w_hi)) for k in range(CH)]
                    for n, (v, w_, k) in enumerate(trio):
                        if t == 0 and v is h_lo and k == 0 and s < STEPS - 1:
                            pe.wait_ge(h_lo_ready, s + 1)
                        if t == 0 and v is h_lo and s == STEPS - 1:
                            pe.wait_ge(h_lo_last, k + 1)
                        last = nc.tensor.matmul(dst, v[:, s % (LAG + 1), k, t * P:(t + 1) * P], w_[:, e, 1, k, :],
                                                start=n == 0, stop=n == len(trio) - 1)
                    if t == TILES - 1 or s == STEPS - 1:
                        last.then_inc(y_ready, 1)

            similarities()
            transpose_masked(0)
            keep_busy(12)
            transpose_xn(0)
            keep_busy(3)
            for s in range(STEPS + LAG):
                b, e = divmod(s, EXPERTS)
                more = b + 1 < BATCHES
                if more and e == 7:
                    transpose_xn(b + 1)
                if s < STEPS:
                    up(s)
                    if e == 0:
                        gate(b)
                    if e == 1:
                        turn_logits(b)
                    if e == 4:
                        transpose_comb(b)
                    if e == 7:
                        bias_sums(b)
                if more and e == 2:
                    sum_missed(b + 1)
                if more and e == 5:
                    transpose_masked(b + 1)
                if s >= LAG:
                    down(s - LAG)

        @block.scalar
        def _(act):
            def u_copy(b):
                act.wait_ge(u_ready, b + 1)
                nc.scalar.activation(u_sb[:, b * N:(b + 1) * N], U_BANKS[b][0:D, 0:N], ACT.Copy,
                                     scale=SIM_SCALE).then_inc(u_copied, 1)

            def sim_copy(b):
                for t in range(TILES if b else 1):
                    act.wait_ge(sim_ready, (b + 1) * TILES if b else 1)
                    nc.scalar.activation(sim[:, b, t], tiled(SIM_BANKS[b][t])[:, t, :], ACT.Copy,
                                         accum_out=row_sum[:, b, t:t + 1]).then_inc(sim_copied, 1)

            def spread_of(b):
                for t in range(TILES):
                    wait_for_sim(act, b, t)
                    nc.scalar.activation(act_waste[:, t], sim[:, b, t], ACT.Abs, scale=-float(N),
                                         bias=row_sum[:, b, t:t + 1],
                                         accum_out=spread[:, b, t:t + 1]).then_inc(spread_ready, 1)

            def signs_of(b):
                for t in range(TILES):
                    act.wait_ge(guess_ready, b * TILES + t + 1)
                    nc.scalar.activation(act_waste[:, t], sim[:, b, t], ACT.Sign, bias=neg_guess[:, b, t:t + 1],
                                         accum_out=signs[:, b, t:t + 1]).then_inc(signs_ready, 1)

            def sigmoid(b):
                nc.scalar.activation(half[:, b], sim[:, b], ACT.Tanh, scale=0.5).then_inc(sig_th, 1)
                act.wait_ge(sig_th, b + 1)
                if b == 0:
                    act.wait_ge(gam_ready, 1)
                nc.scalar.activation(half[:, b], half[:, b], ACT.Identity, scale=gam[:, 1:2],
                                     bias=gam[:, 1:2]).then_inc(sig_ready, 1)

            def weight_hi(e):
                act.wait_ge(w_in[e], 16)
                nc.scalar.activation(w_hi[:, e], w_sb[:, e], ACT.Copy).then_inc(w_hi_ready, 1)

            def xt_hi_of(b):
                if b >= 2:
                    act.wait_ge(h_ready, (b - 1) * EXPERTS)
                for k in range(CH):
                    act.wait_ge(xn_t, b * CH + k + 1)
                    nc.scalar.activation(xt_hi[:, b % 2, k], XT_BANKS[k][:, 0:N], ACT.Copy).then_inc(xt_hi_ready, 1)

            def gelu(s):
                b, e = divmod(s, EXPERTS)
                act.wait_ge(h_ready, s + 1)
                if s >= 2:
                    act.wait_ge(h_lo_ready, s - 1)
                for c in range(CH):
                    last = nc.scalar.activation(h_act[:, s % 2, c], tiled(p_h[s % 2])[:, c, :], ACT.Gelu,
                                                bias=b1_sb[:, e, c:c + 1])
                last.then_inc(h_act_ready, 1)

            def hidden_hi(s):
                act.wait_ge(h_act_ready, s + 1)
                if s > LAG:
                    act.wait_ge(y_ready, s - LAG)
                nc.scalar.activation(h_hi[:, s % (LAG + 1)], h_act[:, s % 2], ACT.Copy).then_inc(h_hi_ready, 1)

            def comb_hi_of(b):
                act.wait_ge(comb_tr, b + 1)
                nc.scalar.activation(comb_hi[:], COMB_T, ACT.Copy).then_inc(comb_hi_ready, 1)

            nc.scalar.preload_act_table(ACT.Gelu)
            act.wait_ge(m_ready, 1)
            nc.scalar.activation(m_sb[:], p_g[0:D, 0:D], ACT.Copy).then_inc(m_copied, 1)
            u_copy(0)
            act.wait_ge(small_in, 16)
            nc.scalar.activation(gam[:, 0:1], gamma_sb, ACT.Tanh, scale=0.5).then_inc(gam_th, 1)
            sim_copy(0)
            spread_of(0)
            signs_of(0)
            u_copy(BATCHES - 1)
            weight_hi(EARLY)
            sigmoid(0)
            weight_hi(EARLY + 1)
            nc.scalar.activation(gate_parts[:, :, 0], gate_sb, ACT.Copy).then_inc(gate_hi_ready, 1)
            for b in range(1, BATCHES):
                sim_copy(b)
                weight_hi(EARLY + 1 + b)
            weight_hi(EARLY + BATCHES + 1)
            spread_of(1)
            act.wait_ge(b2_in, 16)
            nc.scalar.activation(b2_hi[:], b2_sb[:], ACT.Copy).then_inc(b2_hi_ready, 1)
            xt_hi_of(0)
            for e in range(EARLY + BATCHES + 2, EXPERTS):
                weight_hi(e)
            signs_of(1)
            for s in range(STEPS):
                b, e = divmod(s, EXPERTS)
                more = b + 1 < BATCHES
                if e == 7 and more:
                    xt_hi_of(b + 1)
                gelu(s)
                if e == 0:
                    act.wait_ge(logits_t_ready, b + 1)
                    nc.scalar.activation(logits_t[:], LOGITS_T, ACT.Copy).then_inc(logits_t_copied, 1)
                hidden_hi(s)
                if e == 1:
                    act.wait_ge(gap_ready, b + 1)
                    nc.scalar.activation(gap_th[:], gap[:], ACT.Tanh, scale=0.5).then_inc(gap_th_ready, 1)
                if e == 2 and more:
                    sigmoid(b + 1)
                if e == 4:
                    comb_hi_of(b)
                if e == 5 and b + 2 < BATCHES:
                    spread_of(b + 2)
                if e == 7 and b + 2 < BATCHES:
                    signs_of(b + 2)

        @block.gpsimd
        def _(pool):
            def rstd(veps, rs, b, veps_ready, ready):
                pool.wait_ge(veps_ready, b + 1)
                nc.gpsimd.tensor_tensor(rs[:, b, :], veps[:, b, :], neg_half[:], ALU.pow).then_inc(ready, 1)

            def weight_lo(e, matrices=(0, 1)):
                if e < EARLY:
                    pool.wait_ge(w_hi_early, e + 1)
                else:
                    pool.wait_ge(w_hi_ready, e - EARLY + 1)
                for j in matrices:
                    nc.gpsimd.tensor_tensor(w_lo[:, e, j], w_sb[:, e, j], w_hi[:, e, j],
                                            ALU.subtract).then_inc(w_lo_ready[e][j], 1)

            def base(b):
                pool.wait_ge(ln1_mul, b + 1)
                for t in range(TILES):
                    last = nc.gpsimd.tensor_scalar(x_sb[:, b, t], x_sb[:, b, t], mul1[:, b, t:t + 1],
                                                   add1[:, b, t:t + 1], ALU.mult, ALU.add)
                last.then_inc(base_ready, 1)

            def add_masked(b):
                pool.wait_ge(masked, (b + 1) * TILES)
                pool.wait_ge(base_ready, b + 1)
                nc.gpsimd.tensor_tensor(x_sb[:, b], x_sb[:, b], half[:, b], ALU.add).then_inc(base_sum, 1)

            def hidden_lo(s):
                pool.wait_ge(h_hi_ready, s + 1)
                if s > LAG:
                    pool.wait_ge(y_ready, s - LAG)
                nc.gpsimd.tensor_tensor(h_lo[:, s % (LAG + 1)], h_act[:, s % 2], h_hi[:, s % (LAG + 1)],
                                        ALU.subtract).then_inc(h_lo_ready, 1)

            nc.gpsimd.memset(neg_half[:], -0.5).then_inc(const_set, 1)
            nc.gpsimd.memset(ones[:], 1.0).then_inc(const_set, 1)
            pool.wait_ge(const_set, 2)
            rstd(veps1, rstd1, 0, ln1_veps, ln1_rstd)
            base(0)
            for e in range(BEFORE_LN2):
                weight_lo(e)
            pool.wait_ge(gate_hi_ready, 1)
            nc.gpsimd.tensor_tensor(gate_parts[:, :, 1], gate_sb, gate_parts[:, :, 0], ALU.subtract).then_inc(
                gate_lo_ready, 1)
            rstd(veps2, rstd2, 0, ln2_veps, ln2_rstd)
            for e in range(BEFORE_LN2, DVE_SPLITS[0]):
                weight_lo(e)
            for s in range(STEPS):
                b, e = divmod(s, EXPERTS)
                more = b + 1 < BATCHES
                if s < STEPS - 1:
                    hidden_lo(s)
                if more and e == 0:
                    rstd(veps1, rstd1, b + 1, ln1_veps, ln1_rstd)
                if more and e == 2:
                    base(b + 1)
                if more and e == 3:
                    add_masked(b + 1)
                if more and e == 5:
                    rstd(veps2, rstd2, b + 1, ln2_veps, ln2_rstd)
                if s == 5:
                    weight_lo(DVE_SPLITS[0], matrices=(1,))
                if s == 7:
                    weight_lo(DVE_SPLITS[1], matrices=(1,))

        @block.vector
        def _(dve):
            def moments(rows, stats_, mv, veps, stats_ready, agg_ready, veps_ready, b, rows_ready=None):
                for t in range(TILES):
                    if rows_ready is not None:
                        dve.wait_ge(rows_ready, b * TILES + t + 1)
                    nc.vector.bn_stats(stats_[:, t, :], rows[:, b, t]).then_inc(stats_ready, 1)
                for t in range(TILES):
                    dve.wait_ge(stats_ready, b * TILES + t + 1)
                    nc.vector.bn_aggr(mv[:, b, t, :], stats_[:, t, :]).then_inc(agg_ready, 1)
                dve.wait_ge(agg_ready, (b + 1) * TILES)
                nc.vector.tensor_scalar(veps[:, b, :], mv[:, b, :, 1], LN_EPS, None, ALU.add).then_inc(veps_ready, 1)

            def hidden_lo(s):
                for k in range(CH):
                    dve.wait_ge(h_hi_ready, s + 1)
                    dve.wait_ge(y_ready, s - LAG)
                    nc.vector.tensor_tensor(h_lo[:, s % (LAG + 1), k], h_act[:, s % 2, k], h_hi[:, s % (LAG + 1), k],
                                            ALU.subtract).then_inc(h_lo_last, 1)

            def ln1(b):
                dve.wait_ge(x_in[min(b, 1)], 16)
                moments(x_sb, stats, mv1, veps1, ln1_stats, ln1_agg, ln1_veps, b)

            def ln1_affine(b):
                dve.wait_ge(ln1_rstd, b + 1)
                nc.vector.tensor_scalar(mul1[:, b, :], rstd1[:, b, :], gam[:, 2:3], 1.0, ALU.mult, ALU.add)
                nc.vector.scalar_tensor_tensor(add1[:, b, :], mv1[:, b, :, 0], gam[:, 3:4], rstd1[:, b, :], ALU.mult,
                                               ALU.mult).then_inc(ln1_mul, 1)

            def gamma_terms():
                dve.wait_ge(gam_th, 1)
                nc.vector.tensor_scalar(gam[:, 1:2], gam[:, 0:1], 0.125, 0.125, ALU.mult, ALU.add)
                nc.vector.tensor_scalar(gam[:, 2:3], gam[:, 0:1], -0.5, 0.5, ALU.mult, ALU.add)
                nc.vector.tensor_scalar(gam[:, 3:4], gam[:, 0:1], 0.5, -0.5, ALU.mult, ALU.add).then_inc(gam_ready, 1)
                dve.wait_ge(gam_ready, 1)

            def weight_hi(e):
                dve.wait_ge(w_in[e], 16)
                nc.vector.tensor_copy(w_hi[:, e], w_sb[:, e]).then_inc(w_hi_early, 1)

            def weight_lo(e):
                dve.wait_ge(w_hi_ready, e - EARLY + 1)
                nc.vector.tensor_tensor(w_lo[:, e, 0], w_sb[:, e, 0], w_hi[:, e, 0],
                                        ALU.subtract).then_inc(w_lo_ready[e][0], 1)

            def u_copy(b):
                dve.wait_ge(u_ready, b + 1)
                nc.vector.tensor_scalar(u_sb[:, b * N:(b + 1) * N], U_BANKS[b][0:D, 0:N], SIM_SCALE, None,
                                        ALU.mult).then_inc(u_mid_copied, 1)

            def sim_copy(t):
                dve.wait_ge(sim_ready, t + 1)
                nc.vector.tensor_scalar(sim[:, 0, t], tiled(SIM_BANKS[0][t])[:, t, :], 1.0, None, ALU.mult, ALU.add,
                                        accum_out=row_sum[:, 0, t:t + 1]).then_inc(sim0_copied, 1)

            def mean(b, t):
                wait_for_sim(dve, b, t)
                nc.vector.tensor_scalar(neg_mean[:, t:t + 1], row_sum[:, b, t:t + 1], -1.0 / N, None,
                                        ALU.mult).then_inc(mean_ready, 1)

            def first_guess(b, t):
                dve.wait_ge(mean_ready, b * TILES + t + 1)
                dve.wait_ge(spread_ready, b * TILES + t + 1)
                nc.vector.scalar_tensor_tensor(neg_guess[:, b, t:t + 1], spread[:, b, t:t + 1], -Z * SIGMA,
                                               neg_mean[:, t:t + 1], ALU.mult, ALU.add).then_inc(guess_ready, 1)

            def better_guess(b, t):
                dve.wait_ge(signs_ready, b * TILES + t + 1)
                nc.vector.scalar_tensor_tensor(off[:, t:t + 1], signs[:, b, t:t + 1], N - 2 * MIDDLE,
                                               spread[:, b, t:t + 1], ALU.add, ALU.mult).then_inc(off_ready, 1)
                dve.wait_ge(off_ready, b * TILES + t + 1)
                nc.vector.scalar_tensor_tensor(guess[:, t:t + 1], off[:, t:t + 1], PER_COUNT / 2,
                                               neg_guess[:, b, t:t + 1], ALU.mult,
                                               ALU.subtract).then_inc(better_ready, 1)

            def count_above(b, t):
                dve.wait_ge(better_ready, b * TILES + t + 1)
                nc.vector.tensor_scalar(above[:, t], sim[:, b, t], guess[:, t:t + 1], None, ALU.is_ge, ALU.add,
                                        accum_out=count[:, t:t + 1]).then_inc(counted, 1)

            def flag_few(b):
                dve.wait_ge(counted, (b + 1) * TILES)
                nc.vector.tensor_scalar(few[:], count[:], TOP_K - WINDOW, None, ALU.is_lt).then_inc(few_ready, 1)

            def flag_missed(b):
                dve.wait_ge(few_ready, b + 1)
                if b:
                    dve.wait_ge(missed_sum, b)
                nc.vector.scalar_tensor_tensor(missed[:], count[:], TOP_K, few[:], ALU.is_ge, ALU.add).then_inc(
                    missed_ready, 1)

            steps = [0]

            def step_of_tile(ins):
                steps[0] += 1
                ins.then_inc(search, 1)

            def tile_before():
                dve.wait_ge(search, steps[0] - TILES + 1)

            def drop_above(b):
                for t in range(TILES):
                    dve.wait_ge(counted, b * TILES + t + 1)
                    if t == TILES - 1:
                        flag_missed(b)
                    step_of_tile(nc.vector.scalar_tensor_tensor(left[:, t], above[:, t], REPLACED, sim[:, b, t],
                                                                ALU.mult, ALU.add))

            def take_eight(r):
                for t in range(TILES):
                    tile_before()
                    step_of_tile(nc.vector.max(top[:, t, 8 * r:8 * r + 8], left[:, t]))

            def drop_eight(r):
                for t in range(TILES):
                    tile_before()
                    step_of_tile(nc.vector.match_replace(left[:, t], top[:, t, 8 * r:8 * r + 8], left[:, t], REPLACED))

            def choose(b):
                for t in range(TILES):
                    dve.wait_ge(search, steps[0] - TILES + 1 + t)
                    nc.vector.scalar_tensor_tensor(chosen[:, t], above_sb, count[:, t:t + 1], top[:, t, :],
                                                   ALU.is_equal, ALU.mult,
                                                   accum_out=threshold[:, t:t + 1]).then_inc(chosen_ready, 1)

            def know_missed(b):
                dve.wait_ge(missed_sum, b + 1)
                nc.vector.tensor_reduce(any_missed[:, b:b + 1], p_a[0:1, 0:TILES], AX.X, ALU.add).then_inc(
                    missed_known, 1)

            def search_everything(b):
                dve.wait_ge(search, steps[0])
                n = 0
                for r in range(ALL_ROUNDS):
                    last_round = r == ALL_ROUNDS - 1
                    for t in range(TILES):
                        if n >= TILES:
                            dve.wait_ge(search_all[b], n - TILES + 1)
                        nc.vector.max(top[:, t, 0:8] if last_round else top8[:, t],
                                      left[:, t] if r else sim[:, b, t]).then_inc(search_all[b], 1)
                        n += 1
                    for t in range(TILES):
                        if last_round:
                            nc.vector.memset(count[:, t:t + 1], TOP_K - 1 - LAST).then_inc(search_all[b], 1)
                        else:
                            dve.wait_ge(search_all[b], n - TILES + 1)
                            nc.vector.match_replace(left[:, t], top8[:, t], left[:, t] if r else sim[:, b, t],
                                                    REPLACED).then_inc(search_all[b], 1)
                        n += 1
                dve.wait_ge(search_all[b], n)

            def search_again_if_missed(b):
                dve.wait_ge(missed_known, b + 1)
                rows = nc.vector.value_load(any_missed[0:1, b:b + 1].bitcast(I32))
                with nc.vector.If(rows > 0):
                    search_everything(b)

            def mask(b):
                dve.wait_ge(sig_ready, b + 1)
                for t in range(TILES):
                    dve.wait_ge(chosen_ready, b * TILES + t + 1)
                    nc.vector.scalar_tensor_tensor(half[:, b, t], sim[:, b, t], threshold[:, t:t + 1],
                                                   half[:, b, t], ALU.is_ge, ALU.mult).then_inc(masked, 1)

            def add_masked(b):
                dve.wait_ge(base_ready, b + 1)
                for t in range(TILES):
                    dve.wait_ge(masked, b * TILES + t + 1)
                    last = nc.vector.tensor_tensor(x_sb[:, b, t], x_sb[:, b, t], half[:, b, t], ALU.add)
                last.then_inc(base_sum, 1)

            def residual(b):
                dve.wait_ge(masked_t, b + 1)
                dve.wait_ge(base_sum, b + 1)
                for t in range(TILES):
                    nc.vector.tensor_tensor(x1[:, b, t], x_sb[:, b, t], tiled(p_a)[:, t, :], ALU.add).then_inc(
                        x1_ready, 1)
                moments(x1, stats2, mv2, veps2, ln2_stats, ln2_agg, ln2_veps, b, x1_ready)

            def normalise(b):
                dve.wait_ge(ln2_rstd, b + 1)
                if b:
                    dve.wait_ge(xn_t, b * CH)
                for t in range(TILES):
                    nc.vector.tensor_scalar(xn[:, t], x1[:, b, t], mv2[:, b, t, 0:1], rstd2[:, b, t:t + 1],
                                            ALU.subtract, ALU.mult).then_inc(xn_ready, 1)

            def xt_lo_of(b):
                for k in range(CH):
                    dve.wait_ge(xt_hi_ready, b * CH + k + 1)
                    nc.vector.tensor_tensor(xt_lo[:, b % 2, k], XT_BANKS[k][:, 0:N], xt_hi[:, b % 2, k],
                                            ALU.subtract).then_inc(xt_lo_ready, 1)

            gated = [0]

            def step(ins):
                gated[0] += 1
                ins.then_inc(gating, 1)

            def settle():
                dve.wait_ge(gating, gated[0])

            def top2(b):
                dve.wait_ge(logits_ready, b + 1)
                step(nc.vector.tensor_reduce(logits[:], LOGIT_PARTS.rearrange("p t j e -> p t e j"), AX.X, ALU.add))
                settle()
                for t in range(TILES):
                    step(nc.vector.max(best[:, t], logits[:, t]))
                settle()
                nc.vector.tensor_tensor(gap[:], best[:, :, 0], best[:, :, 1], ALU.subtract).then_inc(gap_ready, 1)
                for t in range(TILES):
                    step(nc.vector.max_index(best_at[:, t], best[:, t], logits[:, t]))
                settle()
                step(nc.vector.tensor_copy(best_f[:], best_at[:, :, 0:2]))

            def combine(b):
                by_rank = [P, TILES, 2, EXPERTS]
                by_part = [P, TILES, PARTS, EXPERTS]
                settle()
                step(nc.vector.tensor_tensor(picked[:], iota_sb.unsqueeze(1).unsqueeze(1).to_broadcast(by_rank),
                                             best_f[:].unsqueeze(3).to_broadcast(by_rank), ALU.is_equal))
                dve.wait_ge(gap_th_ready, b + 1)
                step(nc.vector.tensor_scalar(score[:, :, 0], gap_th[:], 0.5, 0.5, ALU.mult, ALU.add))
                step(nc.vector.tensor_scalar(score[:, :, 1], gap_th[:], -0.5, 0.5, ALU.mult, ALU.add))
                settle()
                step(nc.vector.tensor_tensor(picked[:], picked[:], score[:].unsqueeze(3).to_broadcast(by_rank),
                                             ALU.mult))
                settle()
                step(nc.vector.tensor_tensor(weight[:], picked[:, :, 0], picked[:, :, 1], ALU.add))
                settle()
                nc.vector.tensor_tensor(comb[:, b], weight[:].unsqueeze(2).to_broadcast(by_part),
                                        alpha_sb.unsqueeze(1).unsqueeze(1).to_broadcast(by_part),
                                        ALU.mult).then_inc(comb_ready, 1)
                dve.wait_ge(comb_ready, b + 1)

            def comb_parts_of(b):
                dve.wait_ge(comb_hi_ready, b + 1)
                if b:
                    dve.wait_ge(b2_ready, b)
                nc.vector.scalar_tensor_tensor(comb_parts[:], comb_hi[:], split_sb[0:PARTS * EXPERTS, 0:1], COMB_T,
                                               ALU.mult, ALU.add).then_inc(comb_parts_ready, 1)

            def b2_parts_of():
                dve.wait_ge(b2_hi_ready, 1)
                nc.vector.scalar_tensor_tensor(b2_parts[:], b2_hi[:], split_sb[0:PARTS * EXPERTS, 1:2], b2_sb[:],
                                               ALU.mult, ALU.add).then_inc(b2_parts_ready, 1)

            def add_biases(b):
                dve.wait_ge(b2_ready, b + 1)
                dve.wait_ge(y_added, b * EXPERTS + B2_AFTER + 1)
                nc.vector.tensor_tensor(acc[:, b % 2], acc[:, b % 2], tiled(p_s), ALU.add).then_inc(b2_added, 1)

            def add_expert(s):
                b, e = divmod(s, EXPERTS)
                dve.wait_ge(y_ready, s + 1)
                if e:
                    dve.wait_ge(y_added, s)
                elif b >= 2:
                    dve.wait_ge(out_done[b - 2], 16)
                if e == B2_AFTER + 1:
                    dve.wait_ge(b2_added, b + 1)
                for t in range(TILES):
                    if s == STEPS - 1:
                        dve.wait_ge(y_ready, s + 1 + t)
                    so_far = acc[:, b % 2, t] if e else x1[:, b, t]
                    last = nc.vector.scalar_tensor_tensor(acc[:, b % 2, t], tiled(y_bank(s, t))[:, t, :],
                                                          comb[:, b, t, 0, e:e + 1], so_far, ALU.mult, ALU.add)
                    if t == TILES - 1 or s == STEPS - 1:
                        last.then_inc(y_added, 1)

            def guesses(b):
                for t in range(TILES):
                    mean(b, t)
                for t in range(TILES):
                    first_guess(b, t)

            ln1(0)
            gamma_terms()
            ln1_affine(0)
            for e in range(EARLY):
                weight_hi(e)
            mean(0, 0)
            for t in range(1, TILES):
                sim_copy(t)
                mean(0, t)
            first_guess(0, 0)
            u_copy(1)
            for t in range(1, TILES):
                first_guess(0, t)
            u_copy(2)
            for t in range(TILES):
                better_guess(0, t)
                count_above(0, t)
            flag_few(0)
            drop_above(0)
            take_eight(0)
            drop_eight(0)
            take_eight(1)
            know_missed(0)
            drop_eight(1)
            search_again_if_missed(0)
            take_eight(2)
            choose(0)
            mask(0)
            add_masked(0)
            residual(0)
            normalise(0)
            guesses(1)
            xt_lo_of(0)
            ln1(1)
            b2_parts_of()
            weight_lo(DVE_SPLITS[0])
            for s in range(STEPS + LAG):
                b, e = divmod(s, EXPERTS)
                nxt = b + 1
                more = nxt < BATCHES
                if more and e == 0:
                    for t in range(TILES):
                        better_guess(nxt, t)
                    for t in range(TILES):
                        count_above(nxt, t)
                    flag_few(nxt)
                    drop_above(nxt)
                if b < BATCHES and e == 1:
                    top2(b)
                if more and e == 1:
                    take_eight(0)
                    drop_eight(0)
                if b < BATCHES and e == 2:
                    combine(b)
                if more and e == 2:
                    take_eight(1)
                    know_missed(nxt)
                    ln1_affine(nxt)
                if more and e == 3:
                    drop_eight(1)
                    search_again_if_missed(nxt)
                    take_eight(2)
                    choose(nxt)
                    mask(nxt)
                if s == 4:
                    weight_lo(DVE_SPLITS[1])
                if more and e == 5:
                    residual(nxt)
                if more and e == 6:
                    normalise(nxt)
                if b < BATCHES and e == 6:
                    comb_parts_of(b)
                if more and e == 7:
                    xt_lo_of(nxt)
                if e == EXPERTS - 1 and nxt + 1 < BATCHES:
                    guesses(nxt + 1)
                    ln1(nxt + 1)
                if b < BATCHES and e == B2_AFTER + LAG + 1:
                    add_biases(b)
                if s == STEPS:
                    hidden_lo(STEPS - 1)
                if s >= LAG:
                    add_expert(s - LAG)


def kernel(x, ctx_512, L0_xattn_Wq, L0_xattn_Wk, L0_xattn_gamma_raw, L0_ffn_gate_w, L0_ffn_fc1_w, L0_ffn_fc1_b,
           L0_ffn_fc2_w, L0_ffn_fc2_b, L0_ffn_alpha):
    import numpy as np
    import concourse.bacc as bacc
    from concourse.bass_utils import run_bass_kernel_spmd

    B, S, H = x.shape
    T = B * S // P
    E = L0_ffn_fc1_w.shape[0]
    C = H // P

    def rows(w):
        return np.asarray(w).reshape(E, C, P, -1).transpose(2, 0, 1, 3)

    def repeated(a):
        return np.broadcast_to(np.asarray(a, np.float32).reshape(1, -1), (P, np.size(a)))

    third = np.arange(P) // E
    parts = {
        "gamma": repeated(L0_xattn_gamma_raw),
        "alpha": repeated(L0_ffn_alpha),
        "gate_w": np.asarray(L0_ffn_gate_w).reshape(C, P, E).transpose(1, 0, 2).reshape(P, -1),
        "b1": np.asarray(L0_ffn_fc1_b).reshape(E, C, P).transpose(2, 0, 1).reshape(P, -1),
        "identity": np.eye(P, dtype=np.float32),
        "expert": repeated(np.arange(E)),
        "split": -np.stack([third == 1, third == 2], axis=1).astype(np.float32),
        "above": repeated(max(1, int(S * TOP_K_RATIO)) - 1 - np.arange(8 * ROUNDS)),
    }
    arrays = {
        "x": np.asarray(x).reshape(T, P, H).transpose(1, 0, 2),
        "attn": np.concatenate([np.asarray(L0_xattn_Wq), np.asarray(L0_xattn_Wk),
                                np.asarray(ctx_512).reshape(B * S, -1).T], axis=1),
        "small": np.concatenate([parts[name] for name, _ in small_columns(E, C)], axis=1),
        "w": np.stack([rows(L0_ffn_fc1_w), rows(L0_ffn_fc2_w)], axis=2),
        "b2": np.concatenate([np.asarray(L0_ffn_fc2_b)] * 3, axis=0),
    }
    arrays = {k: np.ascontiguousarray(v) for k, v in arrays.items()}
    nc = bacc.Bacc("TRN2", target_bir_lowering=False, num_devices=1)
    aps = {k: nc.dram_tensor(k, v.shape, mybir.dt.from_np(v.dtype), kind="ExternalInput").ap()
           for k, v in arrays.items()}
    out = nc.dram_tensor("out", (P, T, H), F32, kind="ExternalOutput").ap()
    xattn_moe_program(nc, out=out, **aps)
    result = run_bass_kernel_spmd(nc, [arrays], core_ids=[0]).results[0]["out"]
    return np.ascontiguousarray(np.asarray(result).transpose(1, 0, 2)).reshape(B, S, H)
```
